# Optimizing a Trainium2 kernel written in Bass

```python
import numpy as np
import jax
import jax.numpy as jnp

def _softmax(x, axis=-1):
    return jax.nn.softmax(x, axis=axis)

def _gelu(x):
    return jax.nn.gelu(x, approximate=True)

def _silu(x):
    return jax.nn.silu(x)

def _sigmoid(x):
    return jax.nn.sigmoid(x)

def _layernorm(x, axis=-1, eps=1e-05):
    m = jnp.mean(x, axis=axis, keepdims=True)
    v = jnp.var(x, axis=axis, keepdims=True)
    return (x - m) / jnp.sqrt(v + eps)

def _scatter_add(tgt, idx, src, axis=0):
    return tgt.at[idx].add(src)

def _segment_sum(src, seg, n):
    return jax.ops.segment_sum(src, seg, n)
kernel_name = 'mk_adj_resnorm_d2_adj_r2_12ec9a'

def setup_inputs(seed: int=0):
    np.random.seed(seed)
    _w = jnp.asarray

    def _rec_inputs():
        import jax
        import jax.numpy as jnp
        _gk = jax.random.key(seed)
        x = -0.000929 + 1 * jax.random.normal(jax.random.fold_in(_gk, 1), (4096, 128), jnp.float32)
        _a = jax.random.bernoulli(jax.random.fold_in(_gk, 2), 0.000976562, (4096, 4096))
        _a = jnp.logical_or(_a, jnp.eye(4096, dtype=bool))
        _af = _a.astype(jnp.float32)
        _af = _af / jnp.maximum(_af.sum(-1, keepdims=True), 1.0)
        adj = _af
        return (x, adj)
    x, adj = _rec_inputs()

    def _L0_gnn_setup():
        import jax, jax.numpy as jnp
        import numpy as np
        from jax import lax
        D_MODEL = 128
        D_STATE = 16
        D_CONV = 4
        EXPAND = 2
        D_INNER = EXPAND * D_MODEL
        DT_RANK = (D_MODEL + 15) // 16
        N = 2048
        EPS = 1e-05

        def _mamba(h, w_in, conv_w, conv_b, w_xp, w_dt, b_dt, A_log, D_skip, w_out):
            L = h.shape[0]
            xz = h @ w_in
            xc, z = (xz[:, :D_INNER], xz[:, D_INNER:])
            xpad = jnp.pad(xc, ((D_CONV - 1, 0), (0, 0)))
            xconv = sum((xpad[k:k + L] * conv_w[:, k] for k in range(D_CONV))) + conv_b
            u = jax.nn.silu(xconv)
            dbc = u @ w_xp
            dt = jax.nn.softplus(dbc[:, :DT_RANK] @ w_dt + b_dt)
            B = dbc[:, DT_RANK:DT_RANK + D_STATE]
            C = dbc[:, DT_RANK + D_STATE:]
            A = -jnp.exp(A_log)
            dA = jnp.exp(dt[:, :, None] * A[None])
            dBu = dt[:, :, None] * B[:, None, :] * u[:, :, None]

            def step(hst, inp):
                dAt, dBut, Ct = inp
                hst = dAt * hst + dBut
                return (hst, hst @ Ct)
            _, ys = lax.scan(step, jnp.zeros((D_INNER, D_STATE), h.dtype), (dA, dBu, C))
            y = ys + u * D_skip
            y = y * jax.nn.silu(z)
            return y @ w_out
        key = jax.random.key(seed)
        ks = jax.random.split(key, 16)
        x = jax.random.normal(ks[0], (N, D_MODEL), dtype=jnp.float32)
        a = jax.random.uniform(ks[1], (N, N), dtype=jnp.float32)
        adj = a / a.sum(axis=1, keepdims=True)
        s = lambda fi, fo: 1.0 / np.sqrt(fi)
        gcn_w = jax.random.uniform(ks[2], (D_MODEL, D_MODEL), jnp.float32, -s(D_MODEL, 0), s(D_MODEL, 0))
        gcn_b = jnp.zeros((D_MODEL,), jnp.float32)
        ln_g = jnp.ones((D_MODEL,), jnp.float32)
        ln_b = jnp.zeros((D_MODEL,), jnp.float32)
        w_in = jax.random.normal(ks[3], (D_MODEL, 2 * D_INNER), jnp.float32) * s(D_MODEL, 0)
        conv_w = jax.random.normal(ks[4], (D_INNER, D_CONV), jnp.float32) * s(D_CONV, 0)
        conv_b = jnp.zeros((D_INNER,), jnp.float32)
        w_xp = jax.random.normal(ks[5], (D_INNER, DT_RANK + 2 * D_STATE), jnp.float32) * s(D_INNER, 0)
        w_dt = jax.random.normal(ks[6], (DT_RANK, D_INNER), jnp.float32) * s(DT_RANK, 0)
        b_dt = jnp.log(jnp.expm1(jnp.exp(jax.random.uniform(ks[7], (D_INNER,), jnp.float32, np.log(0.001), np.log(0.1)))))
        A_log = jnp.log(jnp.broadcast_to(jnp.arange(1, D_STATE + 1, dtype=jnp.float32), (D_INNER, D_STATE)))
        D_skip = jnp.ones((D_INNER,), jnp.float32)
        w_out = jax.random.normal(ks[8], (D_INNER, D_MODEL), jnp.float32) * s(D_INNER, 0)
        return dict(x=x, adj=adj, gcn_w=gcn_w, gcn_b=gcn_b, ln_g=ln_g, ln_b=ln_b, w_in=w_in, conv_w=conv_w, conv_b=conv_b, w_xp=w_xp, w_dt=w_dt, b_dt=b_dt, A_log=A_log, D_skip=D_skip, w_out=w_out)
    _L0_gnn_all = _L0_gnn_setup()
    _L0_gnn_in = {k: v for k, v in _L0_gnn_all.items() if k in ('gcn_w', 'gcn_b', 'ln_g', 'ln_b', 'w_in', 'conv_w', 'conv_b', 'w_xp', 'w_dt', 'b_dt', 'A_log', 'D_skip', 'w_out')}
    del _L0_gnn_all

    def _L1_gnn_setup():
        import jax, jax.numpy as jnp
        import numpy as np
        N = 4096
        D = 128
        L = 3

        def _cxin_conv(x, a, eps, W, b):
            ax = a @ x
            h = ax + (1.0 + eps[0]) * ax
            for i in range(L):
                h = jax.nn.relu(h @ W[i].T + b[i])
            return h
        key = jax.random.key(seed)
        ks = jax.random.split(key, 8)
        s = 1.0 / np.sqrt(D)
        return {'x1': jax.random.normal(ks[0], (N, D), jnp.float32), 'x2': jax.random.normal(ks[1], (N, D), jnp.float32), 'G1': jax.random.uniform(ks[2], (N, N), jnp.float32), 'G2': jax.random.uniform(ks[3], (N, N), jnp.float32), 'eps1': jnp.zeros((1,), jnp.float32), 'eps2': jnp.zeros((1,), jnp.float32), 'W1': jax.random.normal(ks[4], (L, D, D), jnp.float32) * s, 'b1': jnp.zeros((L, D), jnp.float32), 'W2': jax.random.normal(ks[5], (L, D, D), jnp.float32) * s, 'b2': jnp.zeros((L, D), jnp.float32), 'Wm': jax.random.normal(ks[6], (D, 2 * D), jnp.float32) * (1.0 / np.sqrt(2 * D)), 'bm': jnp.zeros((D,), jnp.float32)}
    _L1_gnn_all = _L1_gnn_setup()
    _L1_gnn_in = {k: v for k, v in _L1_gnn_all.items() if k in ('x2', 'eps1', 'eps2', 'W1', 'b1', 'W2', 'b2', 'Wm', 'bm')}
    del _L1_gnn_all
    return {'x': x, 'adj': adj, 'L0_gnn_gcn_w': _L0_gnn_in['gcn_w'], 'L0_gnn_gcn_b': _L0_gnn_in['gcn_b'], 'L0_gnn_ln_g': _L0_gnn_in['ln_g'], 'L0_gnn_ln_b': _L0_gnn_in['ln_b'], 'L0_gnn_w_in': _L0_gnn_in['w_in'], 'L0_gnn_conv_w': _L0_gnn_in['conv_w'], 'L0_gnn_conv_b': _L0_gnn_in['conv_b'], 'L0_gnn_w_xp': _L0_gnn_in['w_xp'], 'L0_gnn_w_dt': _L0_gnn_in['w_dt'], 'L0_gnn_b_dt': _L0_gnn_in['b_dt'], 'L0_gnn_A_log': _L0_gnn_in['A_log'], 'L0_gnn_D_skip': _L0_gnn_in['D_skip'], 'L0_gnn_w_out': _L0_gnn_in['w_out'], 'L1_gnn_x2': _L1_gnn_in['x2'], 'L1_gnn_eps1': _L1_gnn_in['eps1'], 'L1_gnn_eps2': _L1_gnn_in['eps2'], 'L1_gnn_W1': _L1_gnn_in['W1'], 'L1_gnn_b1': _L1_gnn_in['b1'], 'L1_gnn_W2': _L1_gnn_in['W2'], 'L1_gnn_b2': _L1_gnn_in['b2'], 'L1_gnn_Wm': _L1_gnn_in['Wm'], 'L1_gnn_bm': _L1_gnn_in['bm']}

def reference(x, adj, L0_gnn_gcn_w, L0_gnn_gcn_b, L0_gnn_ln_g, L0_gnn_ln_b, L0_gnn_w_in, L0_gnn_conv_w, L0_gnn_conv_b, L0_gnn_w_xp, L0_gnn_w_dt, L0_gnn_b_dt, L0_gnn_A_log, L0_gnn_D_skip, L0_gnn_w_out, L1_gnn_x2, L1_gnn_eps1, L1_gnn_eps2, L1_gnn_W1, L1_gnn_b1, L1_gnn_W2, L1_gnn_b2, L1_gnn_Wm, L1_gnn_bm):
    import jax
    import jax.numpy as jnp

    def _L0_gnn_ref(x, adj, gcn_w, gcn_b, ln_g, ln_b, w_in, conv_w, conv_b, w_xp, w_dt, b_dt, A_log, D_skip, w_out):
        import jax, jax.numpy as jnp
        import numpy as np
        from jax import lax
        D_MODEL = 128
        D_STATE = 16
        D_CONV = 4
        EXPAND = 2
        D_INNER = EXPAND * D_MODEL
        DT_RANK = (D_MODEL + 15) // 16
        N = 2048
        EPS = 1e-05

        def _mamba(h, w_in, conv_w, conv_b, w_xp, w_dt, b_dt, A_log, D_skip, w_out):
            L = h.shape[0]
            xz = h @ w_in
            xc, z = (xz[:, :D_INNER], xz[:, D_INNER:])
            xpad = jnp.pad(xc, ((D_CONV - 1, 0), (0, 0)))
            xconv = sum((xpad[k:k + L] * conv_w[:, k] for k in range(D_CONV))) + conv_b
            u = jax.nn.silu(xconv)
            dbc = u @ w_xp
            dt = jax.nn.softplus(dbc[:, :DT_RANK] @ w_dt + b_dt)
            B = dbc[:, DT_RANK:DT_RANK + D_STATE]
            C = dbc[:, DT_RANK + D_STATE:]
            A = -jnp.exp(A_log)
            dA = jnp.exp(dt[:, :, None] * A[None])
            dBu = dt[:, :, None] * B[:, None, :] * u[:, :, None]

            def step(hst, inp):
                dAt, dBut, Ct = inp
                hst = dAt * hst + dBut
                return (hst, hst @ Ct)
            _, ys = lax.scan(step, jnp.zeros((D_INNER, D_STATE), h.dtype), (dA, dBu, C))
            y = ys + u * D_skip
            y = y * jax.nn.silu(z)
            return y @ w_out
        h = jax.nn.relu(adj @ x @ gcn_w + gcn_b)
        mu = h.mean(-1, keepdims=True)
        var = h.var(-1, keepdims=True)
        h = (h - mu) * lax.rsqrt(var + EPS) * ln_g + ln_b
        return _mamba(h, w_in, conv_w, conv_b, w_xp, w_dt, b_dt, A_log, D_skip, w_out)

    def _L1_gnn_ref(x1, x2, G1, G2, eps1, eps2, W1, b1, W2, b2, Wm, bm):
        import jax, jax.numpy as jnp
        import numpy as np
        N = 4096
        D = 128
        L = 3

        def _cxin_conv(x, a, eps, W, b):
            ax = a @ x
            h = ax + (1.0 + eps[0]) * ax
            for i in range(L):
                h = jax.nn.relu(h @ W[i].T + b[i])
            return h
        out1 = _cxin_conv(x1, G1, eps1, W1, b1)
        out2 = _cxin_conv(x2, G2, eps2, W2, b2)
        merged = jnp.concatenate((out1, out2), axis=1)
        return merged @ Wm.T + bm
    x = _layernorm(x + _L0_gnn_ref(x, adj, L0_gnn_gcn_w, L0_gnn_gcn_b, L0_gnn_ln_g, L0_gnn_ln_b, L0_gnn_w_in, L0_gnn_conv_w, L0_gnn_conv_b, L0_gnn_w_xp, L0_gnn_w_dt, L0_gnn_b_dt, L0_gnn_A_log, L0_gnn_D_skip, L0_gnn_w_out), axis=-1)
    x = _layernorm(x + _L1_gnn_ref(x, L1_gnn_x2, adj, adj, L1_gnn_eps1, L1_gnn_eps2, L1_gnn_W1, L1_gnn_b1, L1_gnn_W2, L1_gnn_b2, L1_gnn_Wm, L1_gnn_bm), axis=-1)
    return x

_drawn_inputs = setup_inputs


def setup_inputs(seed=0):
    import zlib

    import numpy as np

    out = dict(_drawn_inputs(seed))
    spreads = {'L0_gnn_gcn_b': (0.0, 0.1),
     'L0_gnn_ln_g': (1.0, 0.2),
     'L0_gnn_ln_b': (0.0, 0.1),
     'L0_gnn_conv_b': (0.0, 0.1),
     'L0_gnn_D_skip': (1.0, 0.2),
     'L1_gnn_b1': (0.0, 0.1),
     'L1_gnn_b2': (0.0, 0.1),
     'L1_gnn_bm': (0.0, 0.1)}
    factors = {}
    for name, (base, spread) in spreads.items():
        noise = np.random.default_rng([zlib.crc32(name.encode()), seed]).standard_normal(out[name].shape)
        drawn = base * np.exp(spread * noise) if base else spread * noise
        out[name] = jnp.asarray(drawn.astype(out[name].dtype))
    for name, factor in factors.items():
        out[name] = (out[name] * factor).astype(out[name].dtype)
    return out
```

```python
import concourse.bass as bass
from concourse import mybir
from contextlib import ExitStack

F32 = mybir.dt.float32
BF16 = mybir.dt.bfloat16
ALU = mybir.AluOpType
ACT = mybir.ActivationFunctionType

P = 128
N = 4096
D = 128
T = 512
NC = N // T
JT = T // P
G = 2
S = 16
R = 8
KC = 4
HALO = KC - 1
L = 3
NBLK = N // T
RING = 4
EPS = 1e-5

PACK = {}
_at = 0
for _n, _w in (("gcn_w", D), ("w_in", 4 * P), ("w_xp", G * (R + 2 * S)), ("w_out", G * D),
               ("W1", L * D), ("W2", L * D), ("Wm", 2 * D),
               ("gcn_b", 1), ("ln_g", 1), ("ln_b", 1), ("conv_w", G * KC), ("conv_b", G),
               ("b_dt", G), ("D_skip", G), ("A_log", G * S), ("b1", L), ("b2", L)):
    PACK[_n] = (_at, _at + _w)
    _at += _w
PACK_W = _at


def two_layer_graph_kernel(nc, blocks, xs_d, pack_d, w_dt_d, eps1_d, eps2_d, bm_d, out_d):
    ctx = ExitStack()
    with ctx:
        def sb(name, shape, dt=F32):
            return ctx.enter_context(nc.sbuf_tensor(name, shape, dt))

        def pb(name, shape=(P, T)):
            return ctx.enter_context(nc.psum_tensor(name, list(shape), F32))

        def sem(name):
            return ctx.enter_context(nc.semaphore(name))

        xs = sb("xs", [P, N // P, 2 * D])
        ring = sb("ring", [P, RING, JT, T])
        acc2 = sb("acc2", [P, N])
        resid = sb("resid", [P, N // P, D])
        dt_ = sb("dt", [P, 2, G, T])
        dtu = sb("dtu", [P, 2, G, T])
        gate = sb("gate", [P, 2, G, T])
        y = sb("y", [P, 2, G, T])
        bh = sb("bh", [P, 2, G, T])
        prod = sb("prod", [P, 2, G, T])
        bc = sb("bc", [P, 2, T], BF16)
        state = sb("state", [P, S, G])
        xcv = sb("xcv", [P, G, HALO + T])
        ax = sb("ax", [P, T])
        ax2 = sb("ax2", [P, T])
        hr = sb("hr", [P, T])
        hc = sb("hc", [P, T])
        sq = sb("sq", [P, T])
        u = sb("u", [P, G, T])
        dbc = sb("dbc", [P, T])
        rest = sb("rest", [P, T])
        sp = sb("sp", [P, G, T])
        mb = sb("mb", [P, 2, T])
        yg = sb("yg", [P, G, T])
        r = sb("r", [P, JT, D])
        x1 = sb("x1", [P, JT, D])
        bn6 = sb("bn6", [P, JT, 6])
        mv = sb("mv", [P, JT, 2])
        rstd = sb("rstd", [P, JT])
        pack = sb("pack", [P, PACK_W])
        wx3 = sb("wx3", [P, G, P])
        w_dt = sb("w_dt", [P, G * P])
        A = sb("A", [P, G, S])
        mean_w = sb("mean_w", [P, P])
        sel = sb("sel", [P, 2 * S], BF16)
        bm = sb("bm", [P, D])
        scale1 = sb("scale1", [P, 1])
        scale2 = sb("scale2", [P, 1])
        eps_t = sb("eps_t", [P, 1])

        def w(name):
            return pack[:, PACK[name][0]:PACK[name][1]]

        gcn_w, w_in = w("gcn_w"), w("w_in")
        w_xp = w("w_xp").rearrange("p (g n) -> p g n", g=G)
        w_out = w("w_out").rearrange("p (g n) -> p g n", g=G)
        W1 = w("W1").rearrange("p (l n) -> p l n", l=L)
        W2 = w("W2").rearrange("p (l n) -> p l n", l=L)
        Wm = w("Wm").rearrange("p (b n) -> p b n", b=2)
        conv_w = w("conv_w").rearrange("p (g k) -> p g k", g=G)
        conv_b, b_dt, D_skip, b1, b2 = w("conv_b"), w("b_dt"), w("D_skip"), w("b1"), w("b2")

        p_x = pb("p_x")
        p_x2 = pb("p_x2")
        p_two = pb("p_two")
        p_dA = [pb("p_dA0"), pb("p_dA1")]
        p_B = pb("p_B")
        p_C = pb("p_C")
        p_m = pb("p_m")
        p_m4 = p_m[:, :].rearrange("p (t n) -> p t n", t=JT)

        def both(bank):
            return bank[:, :].rearrange("p (g t) -> p g t", g=1).to_broadcast([P, G, T])

        s_pack, s_wdt, s_consts_in = sem("s_pack"), sem("s_wdt"), sem("s_consts_in")
        s_xs = [sem(f"s_xs{i}") for i in range(NBLK)]
        s_zero, s_sel, s_A = sem("s_zero"), sem("s_sel"), sem("s_A")
        s_mean_w, s_wx3, s_scales, s_tap, s_part = (sem(n) for n in ("s_mean_w", "s_wx3", "s_scales", "s_tap", "s_part"))
        s_blk = [sem(f"s_blk{i}") for i in range(RING)]
        s_blk_used = sem("s_blk_used")
        s_bb, s_cb, s_dA = sem("s_bb"), sem("s_cb"), sem("s_dA")
        s_bmul, s_scan, s_cmul = sem("s_bmul"), sem("s_scan"), sem("s_cmul")
        s_state, s_acc = sem("s_state"), sem("s_acc")
        s_ax, s_ax2, s_gcn, s_hr = (sem(n) for n in ("s_ax", "s_ax2", "s_gcn", "s_hr"))
        s_mu, s_hc, s_sq, s_var, s_ln, s_rs = (sem(n) for n in ("s_mu", "s_hc", "s_sq", "s_var", "s_ln", "s_rs"))
        s_hg, s_h, s_xc, s_halo, s_xcv = (sem(n) for n in ("s_hg", "s_h", "s_xc", "s_halo", "s_xcv"))
        s_z, s_gate, s_conv, s_u, s_dbcp, s_dbc = (sem(n) for n in ("s_z", "s_gate", "s_conv", "s_u", "s_dbcp", "s_dbc"))
        s_yinit, s_split, s_dtp, s_abs, s_sp = (sem(n) for n in ("s_yinit", "s_split", "s_dtp", "s_abs", "s_sp"))
        s_relu, s_dt, s_dtu = (sem(n) for n in ("s_relu", "s_dt", "s_dtu"))
        s_yg, s_o, s_r, s_stats, s_rv, s_x1, s_res = (sem(n) for n in ("s_yg", "s_o", "s_r", "s_stats", "s_rv", "s_x1", "s_res"))
        s_mm2, s_mr2, s_res0, s_two, s_two_add = (sem(n) for n in ("s_mm2", "s_mr2", "s_res0", "s_two", "s_two_add"))
        s_l, s_f, s_mg, s_fr, s_fst, s_fv, s_fo, s_fin = (sem(n) for n in (
            "s_l", "s_f", "s_mg", "s_fr", "s_fst", "s_fv", "s_fo", "s_fin"))
        s_out = [sem("s_out0"), sem("s_out1")]

        def wait(eng, s, value):
            if isinstance(value, int) and value <= 0:
                return
            assert isinstance(value, int) or value.min_val > 0
            eng.wait_ge(s, value)

        FIRST_HALF = NBLK
        EARLY = {8: ["gcn"]}
        LATE = {0: ["gate_y"], 1: ["out"], 2: ["ln_x1"], 3: ["mlp0"], 4: ["mlp1"], 5: ["mlp2"], 6: ["mlp3"],
                8: ["mean"], 9: ["var"], 10: ["in_proj"], 11: ["conv0"], 12: ["conv1", "silu"],
                13: ["x_proj"], 14: ["dt"], 15: ["softplus"]}
        POST = ("gate_y", "out", "ln_x1")
        MLP = ("mlp0", "mlp1", "mlp2", "mlp3")
        PRE = ("gcn", "mean", "var", "in_proj", "conv0", "conv1", "silu", "x_proj", "dt", "softplus")

        def steps(table, unit, c, b):
            for name in table.get(unit, ()):
                if name in POST and not (isinstance(c, int) and c == 0):
                    yield name, c - 1, 1 - b
                elif name in MLP:
                    yield name, c, b
                elif name in PRE and not (isinstance(c, int) and c == NC - 1):
                    yield name, c + 1, 1 - b

        def first_use(c):
            return 4 * c if not (isinstance(c, int) and c == 0) else 2

        def has_one(c):
            return not (isinstance(c, int) and c == NC - 1)

        def has_two(c):
            return not (isinstance(c, int) and c == 0)

        def two_use(c):
            return 4 * c + 2 if has_one(c) else 4 * c

        def chunks(eng, body):
            body(0, 0)
            with eng.Fori(1, NC - 2, 2) as c:
                body(c, 1)
                body(c + 1, 0)
            body(NC - 1, 1)

        def mb4(k):
            return mb[:, k, :].rearrange("p (t n) -> p t n", t=JT)

        def fcount(k, l):
            done = 0
            for t in range(NC + 5):
                for ll in (2, 1, 0):
                    kk = t - 1 - ll
                    if 0 <= kk < NC:
                        done += 1
                        if (kk, ll) == (k, l):
                            return done
            return 0

        def layer_bank(l):
            return (p_dA[0], p_dA[1], p_B)[l]

        def merge_bank(k):
            return (p_C, p_m)[k % 2][:, :].rearrange("p (t n) -> p t n", t=JT)

        def one_done(n):
            if isinstance(n, int):
                return NBLK if n == 0 else (2 * NBLK if n == 1 else 16 * (n - 1) + NBLK)
            return 16 * (n - 1) + NBLK

        def two_done(n, k):
            if isinstance(n, int) and n == NC - 1:
                return 4 * two_use(NC - 1) + NBLK + k + 1
            return 4 * two_use(n + 1) + k + 1

        def two_all(n):
            if isinstance(n, int) and n < 0:
                return 0
            return two_done(n, NBLK - 1)

        block = ctx.enter_context(nc.Block())

        @block.sync
        def _(sp_):
            sp_.dma_start(pack[:, :], pack_d).then_inc(s_pack, 16)
            sp_.wait_ge(s_zero, 1)
            sp_.dma_start(w_dt[0:R, :], w_dt_d).then_inc(s_wdt, 16)
            sp_.dma_start(scale1[:, :], eps1_d).then_inc(s_consts_in, 16)
            sp_.dma_start(scale2[:, :], eps2_d).then_inc(s_consts_in, 16)
            sp_.dma_start(bm[:, :], bm_d).then_inc(s_consts_in, 16)

            def load(slot, rows, cols, used):
                wait(sp_, s_blk_used, used)
                sp_.dma_start(ring[:, slot, :, :], blocks[rows, cols]).then_inc(s_blk[slot], 16)

            for k in range(NBLK):
                sp_.dma_start(xs[:, JT * k:JT * (k + 1), :], xs_d[k]).then_inc(s_xs[k], 16)
                load(k % RING, 0, k, k - RING + 1)

            def body(c, b):
                at = 4 * first_use(c)
                if has_one(c):
                    for k in range(NBLK):
                        load(k % RING, c + 1, k, at + k - RING + 1)
                    at = at + NBLK
                if has_two(c):
                    for k in range(NBLK):
                        load(k % RING, k, c - 1, at + k - RING + 1)

            chunks(sp_, body)
            at = 4 * two_use(NC - 1) + NBLK
            for k in range(NBLK):
                load(k % RING, k, NC - 1, at + k - RING + 1)
            for k in range(NC):
                sp_.wait_ge(s_fin, k + 1)
                sp_.dma_start(out_d[k], mb4(k % 2)).then_inc(s_out[k % 2], 16)
            for q in range(2):
                sp_.wait_ge(s_out[q], 16 * (NC // 2))

        @block.tensor
        def _(pe):
            def broadcast(c, b, unit):
                if unit == 0:
                    pe.wait_ge(s_split, c + 1)
                wait(pe, s_bmul, S * c + unit)
                pe.matmul(p_B[:, :], sel[:, unit:unit + 1].to_broadcast([P, P]), bc[:, b, :],
                          start=True, stop=True).then_inc(s_bb, 1)
                wait(pe, s_cmul, S * c + unit)
                pe.matmul(p_C[:, :], sel[:, S + unit:S + unit + 1].to_broadcast([P, P]), bc[:, b, :],
                          start=True, stop=True).then_inc(s_cb, 1)

            def one(n, k, half, use):
                if k == 0 and half == 0:
                    wait(pe, s_relu, n)
                    wait(pe, s_sp, n)
                if half == 0:
                    pe.wait_ge(s_blk[k % RING], 16 * (use + k // RING + 1))
                for jt in range(2 * half, 2 * half + 2):
                    j = JT * k + jt
                    edge = dict(start=j == 0, stop=j == N // P - 1)
                    pe.matmul(p_x[:, :], xs[:, j, 0:D], ring[:, k % RING, jt, :], **edge)
                    last = pe.matmul(p_x2[:, :], xs[:, j, D:2 * D], ring[:, k % RING, jt, :], **edge)
                if half:
                    last.then_inc(s_blk_used, 1)

            def two(n, k, use, bank=None):
                if k == 0:
                    pe.wait_ge(s_x1, n + 1)
                pe.wait_ge(s_two_add, NBLK * n + k + 1)
                pe.wait_ge(s_blk[k % RING], 16 * (use + k // RING + 1))
                for jt in range(JT):
                    last = pe.matmul(p_two[:, :], x1[:, jt, :], ring[:, k % RING, jt, :],
                                     start=jt == 0, stop=jt == JT - 1)
                last.then_inc(s_blk_used, 1)

            def step(name, n, b):
                if name == "gcn":
                    pe.wait_ge(s_ax, n + 1)
                    wait(pe, s_res0, n)
                    pe.matmul(p_m[:, :], gcn_w, ax[:, :], start=True, stop=True).then_inc(s_gcn, 1)
                elif name == "mean":
                    pe.wait_ge(s_hr, n + 1)
                    pe.matmul(p_x[:, :], mean_w[:, :], hr[:, :], start=True, stop=True).then_inc(s_mu, 1)
                elif name == "var":
                    pe.wait_ge(s_sq, n + 1)
                    pe.wait_ge(s_ax2, n + 1)
                    pe.matmul(p_x2[:, :], mean_w[:, :], sq[:, :], start=True, stop=True).then_inc(s_var, 1)
                elif name == "in_proj":
                    pe.wait_ge(s_h, n + 1)
                    for g, bank in ((0, p_x), (1, p_x2)):
                        pe.matmul(bank[:, :], w_in[:, P * g:P * (g + 1)], hc[:, :],
                                  start=True, stop=True).then_inc(s_xc, 1)
                    pe.matmul(p_m[:, :], w_in[:, P * G:P * (G + 1)], hc[:, :],
                              start=True, stop=True).then_inc(s_z, 1)
                    pe.wait_ge(s_xcv, 2 * n + 1)
                    pe.matmul(p_x[:, :], w_in[:, P * (G + 1):P * (G + 2)], hc[:, :],
                              start=True, stop=True).then_inc(s_z, 1)
                elif name == "x_proj":
                    pe.wait_ge(s_u, n + 1)
                    for g in range(G):
                        last = pe.matmul(p_m[:, :], wx3[:, g, :], u[:, g, :], start=g == 0, stop=g == G - 1)
                    last.then_inc(s_dbcp, 1)
                elif name == "dt":
                    pe.wait_ge(s_dbc, n + 1)
                    pe.wait_ge(s_xcv, 2 * n + 2)
                    for g, bank in ((0, p_x), (1, p_x2)):
                        pe.matmul(bank[:, :], w_dt[:, P * g:P * (g + 1)], dbc[:, :],
                                  start=True, stop=True).then_inc(s_dtp, 1)
                elif name == "out":
                    pe.wait_ge(s_yg, n + 1)
                    if not (isinstance(n, int) and n == NC - 1):
                        pe.wait_ge(s_dbc, n + 2)
                    else:
                        pe.wait_ge(s_res0, NC)
                    for t in range(JT):
                        for g in range(G):
                            last = pe.matmul(p_m4[:, t, :], yg[:, g, P * t:P * (t + 1)], w_out[:, g, :],
                                             start=g == 0, stop=g == G - 1)
                    last.then_inc(s_o, 1)
                elif name == "mlp0":
                    pe.wait_ge(s_ax2, n + 1)
                    wait(pe, s_r, n)
                    pe.wait_ge(s_dbc, n + 1)
                    pe.matmul(p_m[:, :], W2[:, 0, :], ax2[:, :], start=True, stop=True).then_inc(s_mm2, 1)
                elif name in ("mlp1", "mlp2"):
                    l = int(name[3])
                    pe.wait_ge(s_mr2, L * n + l)
                    pe.matmul(p_m[:, :], W2[:, l, :], mb[:, (l - 1) % 2, :], start=True, stop=True).then_inc(s_mm2, 1)
                elif name == "mlp3":
                    pe.wait_ge(s_mr2, L * n + L)
                    for t in range(JT):
                        last = pe.matmul(p_m4[:, t, :], mb[:, 0, P * t:P * (t + 1)], Wm[:, 1, :],
                                         start=True, stop=True)
                    last.then_inc(s_mm2, 1)

            pe.wait_ge(s_pack, 16)
            pe.wait_ge(s_wx3, 1)
            pe.wait_ge(s_mean_w, 1)
            pe.wait_ge(s_sel, 3)
            pe.wait_ge(s_wdt, 16)
            for k in range(NBLK):
                pe.wait_ge(s_xs[k], 16)
                one(0, k, 0, 0)
                one(0, k, 1, 0)
            for name in PRE:
                step(name, 0, 0)

            def body(c, b):
                for unit in range(S):
                    broadcast(c, b, unit)
                    for name, n, nb in steps(EARLY, unit, c, b):
                        step(name, n, nb)
                    k = unit % NBLK
                    if unit < FIRST_HALF:
                        if has_one(c):
                            one(c + 1, k, 0, first_use(c))
                        for name, n, nb in steps(LATE, unit, c, b):
                            step(name, n, nb)
                        if has_one(c):
                            one(c + 1, k, 1, first_use(c))
                    else:
                        if has_two(c):
                            two(c - 1, k, two_use(c))
                        for name, n, nb in steps(LATE, unit, c, b):
                            step(name, n, nb)

            chunks(pe, body)
            step("out", NC - 1, 1)

            for t in range(NC + 5):
                if 0 <= t - 4 < NC:
                    k = t - 4
                    pe.wait_ge(s_f, fcount(k, 2))
                    wait(pe, s_fr, k - 1)
                    for jt in range(JT):
                        last = pe.matmul(merge_bank(k)[:, jt, :], sq[:, P * jt:P * (jt + 1)], Wm[:, 0, :],
                                         start=True, stop=True)
                    last.then_inc(s_mg, 1)
                for l, src in ((2, hc), (1, hr), (0, None)):
                    k = t - 1 - l
                    if 0 <= k < NC:
                        if l:
                            pe.wait_ge(s_f, fcount(k, l - 1))
                            moving = src[:, :]
                        else:
                            pe.wait_ge(s_two_add, NBLK * (NC - 1) + k + 2)
                            wait(pe, s_f, fcount(k - 1, 0))
                            moving = acc2[:, T * k:T * (k + 1)]
                        pe.matmul(layer_bank(l)[:, :], W1[:, l, :], moving, start=True, stop=True).then_inc(s_l, 1)
                if t < NC:
                    two(NC - 1, t, two_use(NC - 1) + 2)

        @block.scalar
        def _(act):
            def decay(c, b, unit):
                if unit == 0:
                    act.wait_ge(s_dt, c + 1)
                for g in range(G):
                    wait(act, s_scan, G * (S * c + unit - 1) + g + 1)
                    act.activation(p_dA[g][:, :], dt_[:, b, g, :], ACT.Exp,
                                   scale=A[:, g, unit:unit + 1]).then_inc(s_dA, 1)

            def save_state(c, unit):
                act.wait_ge(s_scan, G * (S * c + unit + 1))
                act.activation(state[:, unit, :], bh[:, unit % 2, :, T - 1], ACT.Copy).then_inc(s_state, 1)

            def step(name, n, b):
                if name == "gcn":
                    act.wait_ge(s_blk_used, one_done(n))
                    act.activation(ax[:, :], p_x[:, :], ACT.Copy).then_inc(s_ax, 1)
                    wait(act, s_mm2, 4 * (n - 1) + 1)
                    act.activation(ax2[:, :], p_x2[:, :], ACT.Copy).then_inc(s_ax2, 1)
                    act.wait_ge(s_gcn, n + 1)
                    act.activation(hr[:, :], p_m[:, :], ACT.Relu, bias=w("gcn_b")).then_inc(s_hr, 1)
                elif name == "mean":
                    act.wait_ge(s_hc, n + 1)
                    act.activation(sq[:, :], hc[:, :], ACT.Square).then_inc(s_sq, 1)
                elif name == "var":
                    act.wait_ge(s_var, n + 1)
                    act.activation(sq[:, :], p_x2[:, :], ACT.Ln, bias=eps_t[:, :]).then_inc(s_ln, 1)
                    act.wait_ge(s_ln, n + 1)
                    act.activation(sq[:, :], sq[:, :], ACT.Exp, scale=-0.5).then_inc(s_rs, 1)
                elif name == "in_proj":
                    wait(act, s_conv, 2 * n)
                    if isinstance(n, int) and n == 0:
                        act.wait_ge(s_zero, 1)
                    else:
                        act.activation(xcv[:, :, 0:HALO], xcv[:, :, T:T + HALO], ACT.Copy).then_inc(s_halo, 1)
                        act.wait_ge(s_halo, n)
                    for g, bank in ((0, p_x), (1, p_x2)):
                        act.wait_ge(s_xc, G * n + g + 1)
                        act.activation(xcv[:, g, HALO:HALO + T], bank[:, :], ACT.Copy).then_inc(s_xcv, 1)
                elif name == "silu":
                    wait(act, s_yg, n - 1)
                    for g, bank in ((0, p_m), (1, p_x)):
                        act.wait_ge(s_z, G * n + g + 1)
                        act.activation(gate[:, b, g, :], bank[:, :], ACT.Silu).then_inc(s_gate, 1)
                    act.wait_ge(s_conv, 2 * n + 2)
                    act.activation(u[:, :, :], u[:, :, :], ACT.Silu).then_inc(s_u, 1)
                elif name == "x_proj":
                    act.wait_ge(s_dbcp, n + 1)
                    act.activation(dbc[:, :], p_m[:, :], ACT.Copy).then_inc(s_dbc, 1)
                    act.wait_ge(s_u, n + 1)
                    for g in range(G):
                        act.activation(y[:, b, g, :], u[:, g, :], ACT.Copy,
                                       scale=D_skip[:, g:g + 1]).then_inc(s_yinit, 1)
                elif name == "dt":
                    for g, bank in ((0, p_x), (1, p_x2)):
                        act.wait_ge(s_dtp, G * n + g + 1)
                        act.activation(sp[:, g, :], bank[:, :], ACT.Abs, bias=b_dt[:, g:g + 1]).then_inc(s_abs, 1)
                    act.wait_ge(s_abs, 3 * n + 2)
                    act.activation(sp[:, :, :], sp[:, :, :], ACT.Exp, scale=-1.0).then_inc(s_abs, 1)
                    act.wait_ge(s_abs, 3 * n + 3)
                    act.activation(sp[:, :, :], sp[:, :, :], ACT.Ln, bias=1.0).then_inc(s_sp, 1)
                elif name == "ln_x1":
                    act.wait_ge(s_stats, 2 * (n + 1))
                    act.activation(rstd[:, :], mv[:, :, 1], ACT.Ln, bias=eps_t[:, :]).then_inc(s_rv, 1)
                    act.wait_ge(s_rv, 2 * n + 1)
                    act.activation(rstd[:, :], rstd[:, :], ACT.Exp, scale=-0.5).then_inc(s_rv, 1)
                elif name in ("mlp0", "mlp1", "mlp2"):
                    l = int(name[3])
                    act.wait_ge(s_mm2, 4 * n + l + 1)
                    act.activation(mb[:, l % 2, :], p_m[:, :], ACT.Relu, bias=b2[:, l:l + 1],
                                   scale=scale2[:, :] if l == 0 else 1.0).then_inc(s_mr2, 1)

            act.wait_ge(s_pack, 16)
            act.activation(A[:, :, :], w("A_log").rearrange("p (g s) -> p g s", g=G), ACT.Exp).then_inc(s_A, 1)
            act.wait_ge(s_A, 1)
            act.activation(A[:, :, :], A[:, :, :], ACT.Copy, scale=-1.0).then_inc(s_A, 1)
            act.wait_ge(s_scales, 1)
            for name in PRE:
                step(name, 0, 0)
            act.wait_ge(s_A, 2)

            def body(c, b):
                decay(c, b, 0)
                for unit in range(S):
                    for name, n, nb in steps(EARLY, unit, c, b):
                        step(name, n, nb)
                    if unit < S - 1:
                        decay(c, b, unit + 1)
                    save_state(c, unit)
                    for name, n, nb in steps(LATE, unit, c, b):
                        step(name, n, nb)

            chunks(act, body)
            step("ln_x1", NC - 1, 1)
            for t in range(NC + 5):
                for l, dst in ((2, sq), (1, hc), (0, hr)):
                    k = t - 1 - l
                    if 0 <= k < NC:
                        act.wait_ge(s_l, fcount(k, l))
                        if l == 2:
                            wait(act, s_mg, k)
                        act.activation(dst[:, :], layer_bank(l)[:, :], ACT.Relu, bias=b1[:, l:l + 1],
                                       scale=scale1[:, :] if l == 0 else 1.0).then_inc(s_f, 1)
                k = t - 4
                if 0 <= k < NC:
                    act.wait_ge(s_fst, 2 * k + 2)
                    act.activation(rstd[:, :], mv[:, :, 1], ACT.Ln, bias=eps_t[:, :]).then_inc(s_fv, 1)
                    act.wait_ge(s_fv, 2 * k + 1)
                    act.activation(rstd[:, :], rstd[:, :], ACT.Exp, scale=-0.5).then_inc(s_fv, 1)

        @block.vector
        def _(dve):
            def unit_ops(c, b, unit):
                q = unit % 2
                if unit == 0:
                    dve.wait_ge(s_dtu, c + 1)
                wait(dve, s_state, S * c + unit - 1)
                dve.wait_ge(s_bb, S * c + unit + 1)
                dve.tensor_tensor(bh[:, q, :, :], both(p_B), dtu[:, b, :, :], ALU.mult).then_inc(s_bmul, 1)
                dve.wait_ge(s_bmul, S * c + unit + 1)
                for g in range(G):
                    dve.wait_ge(s_dA, G * (S * c + unit) + g + 1)
                    first = 0.0 if isinstance(c, int) and c == 0 else state[:, unit, g:g + 1]
                    dve.tensor_tensor_scan(bh[:, q, g, :], p_dA[g][:, :], bh[:, q, g, :], first,
                                           ALU.mult, ALU.add).then_inc(s_scan, 1)
                wait(dve, s_acc, S * c + unit - 1)
                dve.wait_ge(s_cb, S * c + unit + 1)
                dve.wait_ge(s_scan, G * (S * c + unit + 1))
                dve.tensor_tensor(prod[:, q, :, :], both(p_C), bh[:, q, :, :], ALU.mult).then_inc(s_cmul, 1)

            def conv(n, g):
                if g == 0:
                    wait(dve, s_dtu, n)
                    wait(dve, s_yinit, G * n)
                dve.wait_ge(s_xcv, G * n + g + 1)
                dve.tensor_scalar(u[:, g, :], xcv[:, g, 0:T], conv_w[:, g, 0:1], conv_b[:, g:g + 1],
                                  ALU.mult, ALU.add).then_inc(s_tap, 1)
                for k in range(1, KC):
                    dve.wait_ge(s_tap, (KC - 1) * (G * n + g) + k)
                    dve.scalar_tensor_tensor(out=u[:, g, :], in0=xcv[:, g, k:k + T], scalar=conv_w[:, g, k:k + 1],
                                             in1=u[:, g, :], op0=ALU.mult, op1=ALU.add
                                             ).then_inc(s_tap if k < KC - 1 else s_conv, 1)

            def add_two(n, k):
                dve.wait_ge(s_blk_used, two_done(n, k))
                dve.tensor_tensor(acc2[:, T * k:T * (k + 1)], p_two[:, :], acc2[:, T * k:T * (k + 1)],
                                  ALU.add).then_inc(s_two_add, 1)

            def statistics(src, s_st, n):
                for t in range(JT):
                    last = dve.bn_stats(bn6[:, t, :], src[:, t, :])
                last.then_inc(s_st, 1)
                dve.wait_ge(s_st, 2 * n + 1)

            def aggregate(s_st):
                for t in range(JT):
                    last = dve.bn_aggr(mv[:, t, :], bn6[:, t, :])
                last.then_inc(s_st, 1)

            def normalise(src, dst, s_v, s_done, n):
                dve.wait_ge(s_v, 2 * n + 2)
                for t in range(JT):
                    last = dve.tensor_scalar(dst[:, t, :], src[:, t, :], mv[:, t, 0:1], rstd[:, t:t + 1],
                                             ALU.subtract, ALU.mult)
                last.then_inc(s_done, 1)

            def step(name, n, b):
                if name == "mean":
                    dve.wait_ge(s_mu, n + 1)
                    dve.tensor_tensor(hc[:, :], hr[:, :], p_x[:, :], ALU.subtract).then_inc(s_hc, 1)
                elif name == "var":
                    dve.wait_ge(s_rs, n + 1)
                    dve.scalar_tensor_tensor(out=hc[:, :], in0=hc[:, :], scalar=w("ln_g"), in1=sq[:, :],
                                             op0=ALU.mult, op1=ALU.mult).then_inc(s_hg, 1)
                    dve.wait_ge(s_hg, n + 1)
                    dve.tensor_scalar(hc[:, :], hc[:, :], w("ln_b"), None, ALU.add).then_inc(s_h, 1)
                elif name in ("conv0", "conv1"):
                    conv(n, int(name[4]))
                elif name == "x_proj":
                    dve.wait_ge(s_dbc, n + 1)
                    part = bc[:, b, :]
                    chain = [4 * n]

                    def link(ins):
                        ins.then_inc(s_part, 1)
                        chain[0] = chain[0] + 1
                        dve.wait_ge(s_part, chain[0])

                    link(dve.tensor_copy(part, dbc[:, :]))
                    link(dve.tensor_tensor(rest[:, :], dbc[:, :], part, ALU.subtract))
                    link(dve.tensor_copy(bc[64:128, b, :], rest[64:128, :]))
                    link(dve.tensor_tensor(rest[96:128, :], rest[96:128, :], bc[96:128, b, :], ALU.subtract))
                    dve.tensor_copy(bc[96:128, b, :], rest[96:128, :]).then_inc(s_split, 1)
                elif name == "dt":
                    for g, bank in ((0, p_x), (1, p_x2)):
                        dve.wait_ge(s_abs, 3 * n + g + 1)
                        last = dve.tensor_scalar(dt_[:, b, g, :], bank[:, :], b_dt[:, g:g + 1], 0.0,
                                                 ALU.add, ALU.max)
                    last.then_inc(s_relu, 1)
                elif name == "softplus":
                    dve.wait_ge(s_sp, n + 1)
                    dve.wait_ge(s_relu, n + 1)
                    dve.tensor_tensor(dt_[:, b, :, :], dt_[:, b, :, :], sp[:, :, :], ALU.add).then_inc(s_dt, 1)
                elif name == "out":
                    dve.wait_ge(s_o, n + 1)
                    dve.tensor_tensor(r[:, :, :], p_m4, xs[:, bass.ds(JT * n, JT), 0:D], ALU.add).then_inc(s_r, 1)
                    dve.wait_ge(s_r, n + 1)
                    statistics(r, s_stats, n)
                elif name == "ln_x1":
                    aggregate(s_stats)
                    wait(dve, s_blk_used, two_all(n - 1))
                    normalise(r, x1, s_rv, s_x1, n)
                    dve.wait_ge(s_res0, n + 1)
                    dve.wait_ge(s_x1, n + 1)
                    tiles = resid[:, bass.ds(JT * n, JT), :]
                    dve.tensor_tensor(tiles, tiles, x1[:, :, :], ALU.add).then_inc(s_res, 1)
                elif name == "mlp3":
                    dve.wait_ge(s_mm2, 4 * n + 4)
                    dve.tensor_tensor(resid[:, bass.ds(JT * n, JT), :], p_m4,
                                      bm[:, :].rearrange("p (t n) -> p t n", t=1).to_broadcast([P, JT, D]),
                                      ALU.add).then_inc(s_res0, 1)

            dve.memset(eps_t[:, :], EPS)
            dve.wait_ge(s_consts_in, 48)
            dve.tensor_scalar(scale1[:, :], scale1[:, :], 1.0, 1.0, ALU.add, ALU.add)
            dve.tensor_scalar(scale2[:, :], scale2[:, :], 1.0, 1.0, ALU.add, ALU.add).then_inc(s_scales, 1)
            dve.wait_ge(s_two_add, 1)
            dve.wait_ge(s_pack, 16)
            for name in PRE:
                step(name, 0, 0)

            def body(c, b):
                for unit in range(S):
                    for name, n, nb in steps(EARLY, unit, c, b):
                        step(name, n, nb)
                    unit_ops(c, b, unit)
                    if unit >= FIRST_HALF and has_two(c):
                        add_two(c - 1, unit - FIRST_HALF)
                    for name, n, nb in steps(LATE, unit, c, b):
                        step(name, n, nb)

            chunks(dve, body)
            step("out", NC - 1, 1)
            step("ln_x1", NC - 1, 1)
            for t in range(NC + 6):
                if t < NC:
                    add_two(NC - 1, t)
                k = t - 5
                if 0 <= k < NC:
                    if k >= 2:
                        dve.wait_ge(s_out[k % 2], 16 * (k // 2))
                    normalise(r, mb4(k % 2), s_fv, s_fin, k)
                k = t - 4
                if 0 <= k < NC:
                    wait(dve, s_fin, k)
                    dve.wait_ge(s_mg, k + 1)
                    dve.tensor_tensor(r[:, :, :], merge_bank(k), resid[:, JT * k:JT * (k + 1), :],
                                      ALU.add).then_inc(s_fr, 1)
                    dve.wait_ge(s_fr, k + 1)
                    statistics(r, s_fst, k)
                    aggregate(s_fst)

        @block.gpsimd
        def _(pool):
            def add_product(c, b, unit):
                if unit == 0:
                    pool.wait_ge(s_yinit, G * (c + 1))
                pool.wait_ge(s_cmul, S * c + unit + 1)
                wait(pool, s_acc, S * c + unit)
                pool.tensor_tensor(y[:, b, :, :], y[:, b, :, :], prod[:, unit % 2, :, :],
                                   ALU.add).then_inc(s_acc, 1)

            def step(name, n, b):
                if name == "softplus":
                    pool.wait_ge(s_dt, n + 1)
                    pool.wait_ge(s_u, n + 1)
                    pool.tensor_tensor(dtu[:, b, :, :], dt_[:, b, :, :], u[:, :, :], ALU.mult).then_inc(s_dtu, 1)
                elif name == "gate_y":
                    pool.wait_ge(s_acc, S * (n + 1))
                    pool.wait_ge(s_gate, G * (n + 1))
                    pool.tensor_tensor(yg[:, :, :], y[:, b, :, :], gate[:, b, :, :], ALU.mult).then_inc(s_yg, 1)
                elif name == "ln_x1":
                    pool.wait_ge(s_o, n + 1)

            pool.memset(w_dt[:, :], 0.0)
            pool.memset(xcv[:, :, 0:HALO], 0.0)
            pool.memset(sel[:, :], 0.0)
            pool.memset(wx3[:, :, :], 0.0).then_inc(s_zero, 1)
            pool.memset(acc2[:, :], 0.0).then_inc(s_two_add, 1)
            pool.memset(mean_w[:, :], 1.0 / D).then_inc(s_mean_w, 1)
            pool.wait_ge(s_zero, 1)
            for q in range(1, 4):
                if q > 1:
                    pool.wait_ge(s_sel, q - 1)
                pool.affine_select(out=sel[:, :], in_=sel[:, :], compare_op=ALU.not_equal, fill=1.0,
                                   base=-2 * S * q, pattern=[[-1, 2 * S]], channel_multiplier=1).then_inc(s_sel, 1)
            pool.wait_ge(s_pack, 16)
            pool.tensor_copy(wx3[:, :, 0:R], w_xp[:, :, 0:R])
            for q in range(1, 4):
                last = pool.tensor_copy(wx3[:, :, 2 * S * q:2 * S * (q + 1)], w_xp[:, :, R:R + 2 * S])
            last.then_inc(s_wx3, 1)
            for name in PRE:
                step(name, 0, 0)

            def body(c, b):
                for unit in range(S):
                    add_product(c, b, unit)
                    for name, n, nb in steps(LATE, unit, c, b):
                        step(name, n, nb)

            chunks(pool, body)
            step("gate_y", NC - 1, 1)
            step("ln_x1", NC - 1, 1)


def kernel(**inputs):
    import numpy as np
    import concourse.bacc as bacc
    from concourse.bass_utils import run_bass_kernel_spmd as run

    a = {k.replace("L0_gnn_", "").replace("L1_gnn_", ""): np.asarray(v) for k, v in inputs.items()}

    def rows(m):
        m = m.reshape(m.shape[0], -1)
        return m.reshape(-1, P, m.shape[1]).transpose(1, 0, 2).reshape(P, -1)

    parts = {
        "gcn_w": a["gcn_w"], "w_in": a["w_in"], "w_xp": rows(a["w_xp"]), "w_out": rows(a["w_out"]),
        "W1": a["W1"].transpose(2, 0, 1).reshape(D, -1), "W2": a["W2"].transpose(2, 0, 1).reshape(D, -1),
        "Wm": rows(a["Wm"].T), "gcn_b": rows(a["gcn_b"]), "ln_g": rows(a["ln_g"]), "ln_b": rows(a["ln_b"]),
        "conv_w": rows(a["conv_w"]), "conv_b": rows(a["conv_b"]), "b_dt": rows(a["b_dt"]),
        "D_skip": rows(a["D_skip"]), "A_log": rows(a["A_log"]), "b1": a["b1"].T, "b2": a["b2"].T,
    }
    adj = a["adj"].reshape(NC, T, NBLK, JT, P).transpose(0, 2, 4, 3, 1)
    xs = np.concatenate([a["x"], a["x2"]], axis=1).reshape(NC, JT, P, 2 * D).transpose(0, 2, 1, 3)
    arrays = {
        "adj_blocks": np.ascontiguousarray(adj),
        "xs_tiles": np.ascontiguousarray(xs),
        "pack_w": np.ascontiguousarray(np.concatenate([parts[n] for n in PACK], axis=1)),
        "w_dt_rows": np.ascontiguousarray(a["w_dt"]),
        "eps1_in": np.ascontiguousarray(a["eps1"]), "eps2_in": np.ascontiguousarray(a["eps2"]),
        "bm_in": np.ascontiguousarray(a["bm"]),
    }
    nc = bacc.Bacc("TRN2", target_bir_lowering=False, num_devices=1)
    d = {k: nc.dram_tensor(k, v.shape, F32, kind="ExternalInput").ap() for k, v in arrays.items()}
    out = nc.dram_tensor("out_tiles", (NC, P, JT, D), F32, kind="ExternalOutput").ap()

    def spread(ap):
        return ap.rearrange("(a n) -> a n", a=1).to_broadcast([P, ap.shape[0]])

    two_layer_graph_kernel(nc, d["adj_blocks"], d["xs_tiles"], d["pack_w"], d["w_dt_rows"],
                           spread(d["eps1_in"]), spread(d["eps2_in"]), spread(d["bm_in"]), out)
    res = run(nc, [arrays], core_ids=[0])
    got = res.results[0]["out_tiles"]
    return np.ascontiguousarray(got.transpose(0, 2, 1, 3).reshape(N, D))
```

```python
import concourse.bass as bass
from concourse import mybir
from contextlib import ExitStack

F32 = mybir.dt.float32
BF16 = mybir.dt.bfloat16
ALU = mybir.AluOpType
ACT = mybir.ActivationFunctionType

P = 128
N = 4096
D = 128
T = 512
NC = N // T
JT = T // P
G = 2
S = 16
R = 8
KC = 4
HALO = KC - 1
L = 3
NBLK = N // T
RING = 4
EPS = 1e-5
LOG_EXP = "natural_log_exp_and_others"

PACK = {}
_at = 0
for _n, _w in (("gcn_w", D), ("w_in", 4 * P), ("w_xp", G * (R + 2 * S)), ("w_out", G * D),
               ("W1", L * D), ("W2", L * D), ("Wm", 2 * D),
               ("gcn_b", 1), ("ln_g", 1), ("ln_b", 1), ("conv_w", G * KC), ("conv_b", G),
               ("b_dt", G), ("D_skip", G), ("A_log", G * S), ("b1", L), ("b2", L)):
    PACK[_n] = (_at, _at + _w)
    _at += _w
PACK_W = _at


def two_layer_graph_kernel(nc, blocks, xs_d, pack_d, w_dt_d, eps1_d, eps2_d, bm_d, out_d):
    ctx = ExitStack()
    with ctx:
        def sb(name, shape, dt=F32):
            return ctx.enter_context(nc.sbuf_tensor(name, shape, dt))

        def pb(name, shape=(P, T)):
            return ctx.enter_context(nc.psum_tensor(name, list(shape), F32))

        def sem(name):
            return ctx.enter_context(nc.semaphore(name))

        xs = sb("xs", [P, N // P, 2 * D])
        ring = sb("ring", [P, RING, JT, T])
        acc2 = sb("acc2", [P, N])
        resid = sb("resid", [P, N // P, D])
        dt_ = sb("dt", [P, 2, G, T])
        dtu = sb("dtu", [P, 2, G, T])
        gate = sb("gate", [P, 2, G, T])
        y = sb("y", [P, 2, G, T])
        bh = sb("bh", [P, 2, G, T])
        prod = sb("prod", [P, 2, G, T])
        bc = sb("bc", [P, 2, T], BF16)
        state = sb("state", [P, S, G])
        xcv = sb("xcv", [P, G, HALO + T])
        ax = sb("ax", [P, T])
        ax2 = sb("ax2", [P, T])
        hr = sb("hr", [P, T])
        hc = sb("hc", [P, T])
        sq = sb("sq", [P, T])
        u = sb("u", [P, G, T])
        dbc = sb("dbc", [P, T])
        rest = sb("rest", [P, T])
        sp = sb("sp", [P, G, T])
        mb = sb("mb", [P, 2, T])
        yg = sb("yg", [P, G, T])
        r = sb("r", [P, JT, D])
        x1 = sb("x1", [P, 2, JT, D])
        bn6 = sb("bn6", [P, JT, 6])
        mv = sb("mv", [P, JT, 2])
        rstd = sb("rstd", [P, JT])
        pack = sb("pack", [P, PACK_W])
        wx3 = sb("wx3", [P, G, P])
        w_dt = sb("w_dt", [P, G * P])
        A = sb("A", [P, G, S])
        mean_w = sb("mean_w", [P, P])
        sel = sb("sel", [P, 2 * S], BF16)
        bm = sb("bm", [P, D])
        scale1 = sb("scale1", [P, 1])
        scale2 = sb("scale2", [P, 1])
        eps_t = sb("eps_t", [P, 1])

        def w(name):
            return pack[:, PACK[name][0]:PACK[name][1]]

        gcn_w, w_in = w("gcn_w"), w("w_in")
        w_xp = w("w_xp").rearrange("p (g n) -> p g n", g=G)
        w_out = w("w_out").rearrange("p (g n) -> p g n", g=G)
        W1 = w("W1").rearrange("p (l n) -> p l n", l=L)
        W2 = w("W2").rearrange("p (l n) -> p l n", l=L)
        Wm = w("Wm").rearrange("p (b n) -> p b n", b=2)
        conv_w = w("conv_w").rearrange("p (g k) -> p g k", g=G)
        conv_b, b_dt, D_skip, b1, b2 = w("conv_b"), w("b_dt"), w("D_skip"), w("b1"), w("b2")

        p_x = pb("p_x")
        p_x2 = pb("p_x2")
        p_two = pb("p_two")
        p_dA = [pb("p_dA0"), pb("p_dA1")]
        p_B = pb("p_B")
        p_C = pb("p_C")
        p_m = pb("p_m")
        p_m4 = p_m[:, :].rearrange("p (t n) -> p t n", t=JT)

        def both(bank):
            return bank[:, :].rearrange("p (g t) -> p g t", g=1).to_broadcast([P, G, T])

        s_pack, s_wdt, s_consts_in = sem("s_pack"), sem("s_wdt"), sem("s_consts_in")
        s_xs = [sem(f"s_xs{i}") for i in range(NBLK)]
        s_zero, s_sel, s_A = sem("s_zero"), sem("s_sel"), sem("s_A")
        s_mean_w, s_wx3, s_scales, s_tap, s_part = (sem(n) for n in ("s_mean_w", "s_wx3", "s_scales", "s_tap", "s_part"))
        s_blk = [sem(f"s_blk{i}") for i in range(RING)]
        s_blk_used = sem("s_blk_used")
        s_bb, s_cb, s_dA = sem("s_bb"), sem("s_cb"), sem("s_dA")
        s_bmul, s_scan, s_cmul = sem("s_bmul"), sem("s_scan"), sem("s_cmul")
        s_state, s_acc = sem("s_state"), sem("s_acc")
        s_ax, s_ax2, s_gcn, s_hr = (sem(n) for n in ("s_ax", "s_ax2", "s_gcn", "s_hr"))
        s_mu, s_hc, s_sq, s_var, s_ln, s_rs = (sem(n) for n in ("s_mu", "s_hc", "s_sq", "s_var", "s_ln", "s_rs"))
        s_hg, s_h, s_xc, s_halo, s_xcv, s_zcopy = (sem(n) for n in ("s_hg", "s_h", "s_xc", "s_halo", "s_xcv", "s_zcopy"))
        s_z, s_gate, s_conv, s_u, s_dbcp, s_dbc = (sem(n) for n in ("s_z", "s_gate", "s_conv", "s_u", "s_dbcp", "s_dbc"))
        s_yinit, s_split, s_dtp, s_abs, s_sp = (sem(n) for n in ("s_yinit", "s_split", "s_dtp", "s_abs", "s_sp"))
        s_relu, s_dt, s_dtu = (sem(n) for n in ("s_relu", "s_dt", "s_dtu"))
        s_yg, s_o, s_r, s_stats, s_rv, s_x1, s_res = (sem(n) for n in ("s_yg", "s_o", "s_r", "s_stats", "s_rv", "s_x1", "s_res"))
        s_mm2, s_mr2, s_res0, s_two, s_two_add = (sem(n) for n in ("s_mm2", "s_mr2", "s_res0", "s_two", "s_two_add"))
        s_l, s_f, s_mg, s_fr, s_fst, s_fv, s_fo, s_fin = (sem(n) for n in (
            "s_l", "s_f", "s_mg", "s_fr", "s_fst", "s_fv", "s_fo", "s_fin"))
        s_out = [sem("s_out0"), sem("s_out1")]

        def wait(eng, s, value):
            if isinstance(value, int) and value <= 0:
                return
            assert isinstance(value, int) or value.min_val > 0
            eng.wait_ge(s, value)

        EARLY = {0: ["gate_y"], 8: ["gcn"], 11: ["z0"], 12: ["silu"], 14: ["dt1", "softplus"]}
        LATE = {1: ["out"], 2: ["rstd_x1"], 3: ["ln_x1", "mlp0"], 4: ["mlp1"], 5: ["mlp2"],
                6: ["mlp3"], 7: ["take_ax"], 8: ["mean"], 9: ["var"], 10: ["in_x", "conv0"], 11: ["z1", "conv1"],
                12: ["x_proj"], 13: ["dt0"], 14: ["dt_sum"]}
        POST = ("gate_y", "out", "rstd_x1", "ln_x1")
        MLP = ("mlp0", "mlp1", "mlp2", "mlp3")
        PRE = ("take_ax", "gcn", "mean", "var", "in_x", "z0", "z1", "conv0", "conv1", "silu", "x_proj",
               "dt0", "dt1", "softplus", "dt_sum")
        FILL = {"gcn": 1, "mean": 1, "var": 3, "z1": 4, "x_proj": 1, "dt1": 6}
        Q_STEPS = (10, 14)

        def last_chunk(c, n):
            return isinstance(c, int) and c >= NC - n

        def steps(table, unit, c, b):
            for name in table.get(unit, ()):
                if name in POST and not (isinstance(c, int) and c == 0):
                    yield name, c - 1, 1 - b
                elif name in MLP:
                    yield name, c, b
                elif name in PRE and not last_chunk(c, 1):
                    yield name, c + 1, 1 - b

        def two_units(c):
            if isinstance(c, int) and c < 2:
                return []
            if isinstance(c, int) and c == NC - 2:
                return U6
            if isinstance(c, int) and c == NC - 1:
                return U7
            return [1, 3, 5, 7, 9, 11, 13, 15]

        U6 = [8, 9, 10, 11, 12, 13, 14, 15]
        U7 = [0, 1, 4, 5, 6, 7, 8, 9, 10, 12, 13, 14]
        AFTER = 4

        def two_start(c):
            if isinstance(c, int) and c >= NC - 1:
                return two_start(c - 1) + len(two_units(c - 1))
            return (c - 2) * NBLK if not (isinstance(c, int) and c < 2) else 0

        def one_of(c, unit):
            if unit < S // 2:
                return None if last_chunk(c, 1) else (c + 1, NBLK // 2 + unit // 2)
            return None if last_chunk(c, 2) else (c + 2, (unit - S // 2) // 2)

        def two_of(c, unit):
            units = two_units(c)
            return two_start(c) + units.index(unit) if unit in units else None

        def two_chunks(c, unit):
            if isinstance(c, int):
                return two_of(c, unit) // NBLK, two_of(c, unit) % NBLK
            return c - 2, two_units(c).index(unit)

        TURNS = two_start(NC - 2) + len([u_ for u_ in two_units(NC - 2) if u_ < S // 2])

        def two_bank(i):
            return (p_x, p_x2)[i % 2] if isinstance(i, int) and i >= TURNS else p_two

        def chunk_parity(c, b, unit):
            return two_chunks(c, unit)[0] % 2 if isinstance(c, int) else b

        def sequence(c):
            done = []
            for unit in range(S):
                if unit % 2 == 1 and one_of(c, unit) is not None:
                    done.append((unit, 1))
                if unit in two_units(c):
                    done.append((unit, 2))
            return done

        def started(c):
            if isinstance(c, int):
                return NBLK + NBLK // 2 + sum(len(sequence(k)) for k in range(c))
            return started(2) + 2 * NBLK * (c - 2)

        def place(c, unit, one_or_two):
            at = sequence(c).index((unit | 1 if one_or_two == 1 else unit, one_or_two))
            if isinstance(c, int):
                at = at + started(c)
                return at % RING, at // RING + 1, at + 1
            assert started(2) % RING == 0
            return at % RING, started(2) // RING + (2 * NBLK // RING) * (c - 2) + at // RING + 1, started(c) + at + 1

        def chunks(eng, body):
            body(0, 0)
            body(1, 1)
            with eng.Fori(2, NC - 3, 2) as c:
                body(c, 0)
                body(c + 1, 1)
            body(NC - 2, 0)
            body(NC - 1, 1)

        def mb4(k):
            return mb[:, k, :].rearrange("p (t n) -> p t n", t=JT)

        def fcount(k, l):
            done = 0
            for t in range(NC + 5):
                for ll in (2, 1, 0):
                    kk = t - 1 - ll
                    if 0 <= kk < NC:
                        done += 1
                        if (kk, ll) == (k, l):
                            return done
            return 0

        def layer_bank(l):
            return (p_dA[0], p_dA[1], p_B)[l]

        def merge_bank(k):
            return (p_C, p_m)[k % 2][:, :].rearrange("p (t n) -> p t n", t=JT)

        def one_done(n):
            if isinstance(n, int) and n == 0:
                return NBLK
            return place(n - 1, S // 2 - 1, 1)[2]

        AFTER_AT = started(NC)
        TAIL_AT = AFTER_AT + AFTER
        assert two_start(NC) + AFTER == (NC - 1) * NBLK

        block = ctx.enter_context(nc.Block())

        @block.sync
        def _(sp_):
            def load(at, used, rows, cols):
                wait(sp_, s_blk_used, used)
                sp_.dma_start(ring[:, at, :, :], blocks[rows, cols]).then_inc(s_blk[at], 16)

            for k in range(NBLK):
                sp_.dma_start(xs[:, JT * k:JT * (k + 1), :], xs_d[k]).then_inc(s_xs[k], 16)
                load(k % RING, k - RING + 1, 0, k)
                if k == 1:
                    sp_.dma_start(pack[:, :], pack_d).then_inc(s_pack, 16)
                if k == 3:
                    sp_.wait_ge(s_zero, 1)
                    sp_.dma_start(w_dt[0:R, :], w_dt_d).then_inc(s_wdt, 16)
                    sp_.dma_start(scale1[:, :], eps1_d).then_inc(s_consts_in, 16)
                    sp_.dma_start(scale2[:, :], eps2_d).then_inc(s_consts_in, 16)
                    sp_.dma_start(bm[:, :], bm_d).then_inc(s_consts_in, 16)
            for k in range(NBLK // 2):
                load(k % RING, NBLK + k - RING + 1, 1, k)

            def body(c, b):
                for unit, which in sequence(c):
                    slot, fill, done = place(c, unit, which)
                    if which == 1:
                        load(slot, done - RING, *one_of(c, unit))
                    else:
                        n, k = two_chunks(c, unit)
                        load(slot, done - RING, k, n)

            chunks(sp_, body)
            for i in range(AFTER):
                load((AFTER_AT + i) % RING, AFTER_AT + i - RING + 1, NBLK - AFTER + i, NC - 2)
            for k in range(NBLK):
                load((TAIL_AT + k) % RING, TAIL_AT + k - RING + 1, k, NC - 1)
            for k in range(NC):
                sp_.wait_ge(s_fin, k + 1)
                sp_.dma_start(out_d[k], mb4(k % 2)).then_inc(s_out[k % 2], 16)
            for q in range(2):
                sp_.wait_ge(s_out[q], 16 * (NC // 2))

        @block.tensor
        def _(pe):
            def broadcast_B(c, b, unit):
                if unit == 0:
                    pe.wait_ge(s_split, c + 1)
                wait(pe, s_bmul, S * c + unit)
                pe.matmul(p_B[:, :], sel[:, unit:unit + 1].to_broadcast([P, P]), bc[:, b, :],
                          start=True, stop=True).then_inc(s_bb, 1)

            def broadcast_C(c, b, unit):
                wait(pe, s_cmul, S * c + unit)
                pe.matmul(p_C[:, :], sel[:, S + unit:S + unit + 1].to_broadcast([P, P]), bc[:, b, :],
                          start=True, stop=True).then_inc(s_cb, 1)

            def one(n, k, tiles, slot, fill):
                if k == 0 and tiles[0] == 0:
                    wait(pe, s_ax, n)
                    wait(pe, s_ax2, n)
                if tiles[0] == 0:
                    pe.wait_ge(s_blk[slot], 16 * fill)
                for jt in tiles:
                    j = JT * k + jt
                    edge = dict(start=j == 0, stop=j == N // P - 1)
                    pe.matmul(p_x[:, :], xs[:, j, 0:D], ring[:, slot, jt, :], **edge)
                    last = pe.matmul(p_x2[:, :], xs[:, j, D:2 * D], ring[:, slot, jt, :], **edge)
                if tiles[-1] == JT - 1:
                    last.then_inc(s_blk_used, 1)

            def two(i, n, b, k, slot, fill, tiles=range(JT)):
                if tiles[0] == 0:
                    if k == 0:
                        pe.wait_ge(s_x1, n + 1)
                    if isinstance(i, int) and i >= TURNS:
                        pe.wait_ge(s_two_add, i)
                        if i == TURNS:
                            pe.wait_ge(s_ax, NC)
                            pe.wait_ge(s_ax2, NC)
                    else:
                        pe.wait_ge(s_two_add, i + 1)
                    pe.wait_ge(s_blk[slot], 16 * fill)
                for jt in tiles:
                    last = pe.matmul(two_bank(i)[:, :], x1[:, b, jt, :], ring[:, slot, jt, :],
                                     start=jt == 0, stop=jt == JT - 1)
                if tiles[-1] == JT - 1:
                    last.then_inc(s_blk_used, 1)

            def adjacency(c, b, unit):
                tiles = ()
                if one_of(c, unit) is not None:
                    slot, fill, _ = place(c, unit, 1)
                    cut = 3 if (unit | 1) in two_units(c) else 2
                    tiles = range(cut) if unit % 2 == 0 else range(cut, JT)
                    one(*one_of(c, unit), tiles[:2], slot, fill)
                if unit in two_units(c):
                    n, k = two_chunks(c, unit)
                    args = (two_of(c, unit), n, chunk_parity(c, b, unit), k, *place(c, unit, 2)[:2])
                    if not last_chunk(c, 1) and not last_chunk(c, 2):
                        for q, s_read in ((10, s_xcv), (14, s_relu)):
                            if [u_ for u_ in two_units(c) if u_ > q][:1] == [unit]:
                                pe.wait_ge(s_read, G * (c + 2))
                    if unit == two_units(c)[0] and not last_chunk(c, 1):
                        pe.wait_ge(s_relu, G * (c + 1))
                    if not tiles:
                        two(*args, range(JT // 2))
                for name, n, nb in steps(EARLY, unit, c, b):
                    step(name, n, nb)
                broadcast_C(c, b, unit)
                if tiles[2:]:
                    one(*one_of(c, unit), tiles[2:], slot, fill)
                if unit in two_units(c):
                    two(*args, range(JT // 2, JT) if not tiles else range(JT))

            def two_is_added(c, unit):
                before = [u_ for u_ in two_units(c) if u_ < (unit if not last_chunk(c, 2) else S // 2)]
                wait(pe, s_two_add, two_start(c) + len(before) + 1)

            def step(name, n, b):
                if name == "gcn":
                    pe.wait_ge(s_ax, n + 1)
                    wait(pe, s_res0, n)
                    pe.matmul(p_m[:, :], gcn_w, ax[:, :], start=True, stop=True).then_inc(s_gcn, 1)
                elif name == "mean":
                    pe.wait_ge(s_hr, n + 1)
                    pe.matmul(p_m[:, :], mean_w[:, :], hr[:, :], start=True, stop=True).then_inc(s_mu, 1)
                elif name == "var":
                    pe.wait_ge(s_sq, n + 1)
                    pe.matmul(p_m[:, :], mean_w[:, :], sq[:, :], start=True, stop=True).then_inc(s_var, 1)
                elif name == "in_x":
                    pe.wait_ge(s_h, n + 1)
                    pe.matmul(p_m[:, :], w_in[:, 0:P], hc[:, :], start=True, stop=True).then_inc(s_xc, 1)
                    if not (isinstance(n, int) and n == 0):
                        two_is_added(n - 1, 10)
                    pe.matmul(p_two[:, :], w_in[:, P:2 * P], hc[:, :], start=True, stop=True).then_inc(s_xc, 1)
                elif name in ("z0", "z1"):
                    g = int(name[1])
                    if g == 0:
                        pe.wait_ge(s_xcv, G * n + 1)
                    else:
                        pe.wait_ge(s_zcopy, G * n + 1)
                    pe.matmul(p_m[:, :], w_in[:, P * (G + g):P * (G + g + 1)], hc[:, :],
                              start=True, stop=True).then_inc(s_z, 1)
                elif name == "x_proj":
                    pe.wait_ge(s_u, n + 1)
                    for g in range(G):
                        last = pe.matmul(p_m[:, :], wx3[:, g, :], u[:, g, :], start=g == 0, stop=g == G - 1)
                    last.then_inc(s_dbcp, 1)
                elif name in ("dt0", "dt1"):
                    g = int(name[2])
                    if g == 0:
                        pe.wait_ge(s_dbc, n + 1)
                    elif not (isinstance(n, int) and n == 0):
                        two_is_added(n - 1, 14)
                    else:
                        pe.wait_ge(s_xcv, G)
                    pe.matmul((p_m, p_two)[g][:, :], w_dt[:, P * g:P * (g + 1)], dbc[:, :],
                              start=True, stop=True).then_inc(s_dtp, 1)
                elif name == "out":
                    pe.wait_ge(s_yg, n + 1)
                    if not (isinstance(n, int) and n == NC - 1):
                        pe.wait_ge(s_relu, G * (n + 1) + 1)
                    else:
                        pe.wait_ge(s_res0, NC)
                    for t in range(JT):
                        for g in range(G):
                            last = pe.matmul(p_m4[:, t, :], yg[:, g, P * t:P * (t + 1)], w_out[:, g, :],
                                             start=g == 0, stop=g == G - 1)
                    last.then_inc(s_o, 1)
                elif name == "mlp0":
                    pe.wait_ge(s_ax2, n + 1)
                    if isinstance(n, int) and n == 0:
                        pe.wait_ge(s_relu, 1)
                    else:
                        pe.wait_ge(s_r, n)
                    pe.matmul(p_m[:, :], W2[:, 0, :], ax2[:, :], start=True, stop=True).then_inc(s_mm2, 1)
                elif name in ("mlp1", "mlp2"):
                    l = int(name[3])
                    pe.wait_ge(s_mr2, L * n + l)
                    pe.matmul(p_m[:, :], W2[:, l, :], mb[:, (l - 1) % 2, :], start=True, stop=True).then_inc(s_mm2, 1)
                elif name == "mlp3":
                    pe.wait_ge(s_mr2, L * n + L)
                    for t in range(JT):
                        last = pe.matmul(p_m4[:, t, :], mb[:, 0, P * t:P * (t + 1)], Wm[:, 1, :],
                                         start=True, stop=True)
                    last.then_inc(s_mm2, 1)

            for k in range(NBLK):
                pe.wait_ge(s_xs[k], 16)
                one(0, k, range(JT), k % RING, k // RING + 1)
            pe.wait_ge(s_pack, 16)
            pe.wait_ge(s_wx3, 1)
            pe.wait_ge(s_mean_w, 1)
            pe.wait_ge(s_sel, 3)
            pe.wait_ge(s_wdt, 16)
            tile = 0
            for name in PRE:
                step(name, 0, 0)
                for _ in range(FILL.get(name, 0)):
                    k = tile // JT
                    one(1, k, [tile % JT], k % RING, (NBLK + k) // RING + 1)
                    tile += 1
            assert tile == JT * NBLK // 2

            def body(c, b):
                for unit in range(S):
                    broadcast_B(c, b, unit)
                    adjacency(c, b, unit)
                    for name, n, nb in steps(LATE, unit, c, b):
                        step(name, n, nb)

            chunks(pe, body)

            def after(i):
                at = AFTER_AT + i
                two((NC - 1) * NBLK - AFTER + i, NC - 2, 0, NBLK - AFTER + i, at % RING, at // RING + 1)

            after(0)
            after(1)
            step("out", NC - 1, 1)
            after(2)
            after(3)

            for t in range(NC + 5):
                if 0 <= t - 4 < NC:
                    k = t - 4
                    pe.wait_ge(s_f, fcount(k, 2))
                    wait(pe, s_fr, k - 1)
                    for jt in range(JT):
                        last = pe.matmul(merge_bank(k)[:, jt, :], sq[:, P * jt:P * (jt + 1)], Wm[:, 0, :],
                                         start=True, stop=True)
                    last.then_inc(s_mg, 1)
                for l, src in ((2, hc), (1, hr), (0, None)):
                    k = t - 1 - l
                    if 0 <= k < NC:
                        if l:
                            pe.wait_ge(s_f, fcount(k, l - 1))
                            moving = src[:, :]
                        else:
                            pe.wait_ge(s_two_add, NBLK * (NC - 1) + k + 2)
                            wait(pe, s_f, fcount(k - 1, 0))
                            moving = acc2[:, T * k:T * (k + 1)]
                        pe.matmul(layer_bank(l)[:, :], W1[:, l, :], moving, start=True, stop=True).then_inc(s_l, 1)
                if t < NC:
                    two((NC - 1) * NBLK + t, NC - 1, 1, t, (TAIL_AT + t) % RING, (TAIL_AT + t) // RING + 1)

        @block.scalar
        def _(act):
            def decay(c, b, unit):
                if unit == 0:
                    act.wait_ge(s_dt, c + 1)
                for g in range(G):
                    wait(act, s_scan, G * (S * c + unit - 1) + g + 1)
                    act.activation(p_dA[g][:, :], dt_[:, b, g, :], ACT.Exp,
                                   scale=A[:, g, unit:unit + 1]).then_inc(s_dA, 1)

            def save_state(c, unit):
                act.wait_ge(s_scan, G * (S * c + unit + 1))
                act.activation(state[:, unit, :], bh[:, unit % 2, :, T - 1], ACT.Copy).then_inc(s_state, 1)

            def step(name, n, b):
                if name == "take_ax":
                    act.wait_ge(s_blk_used, one_done(n))
                    wait(act, s_gcn, n)
                    act.activation(ax[:, :], p_x[:, :], ACT.Copy).then_inc(s_ax, 1)
                    wait(act, s_mm2, 4 * (n - 1) + 1)
                    act.activation(ax2[:, :], p_x2[:, :], ACT.Copy).then_inc(s_ax2, 1)
                elif name == "gcn":
                    act.wait_ge(s_gcn, n + 1)
                    act.activation(hr[:, :], p_m[:, :], ACT.Relu, bias=w("gcn_b")).then_inc(s_hr, 1)
                elif name == "mean":
                    act.wait_ge(s_hc, n + 1)
                    act.activation(sq[:, :], hc[:, :], ACT.Square).then_inc(s_sq, 1)
                elif name == "var":
                    act.wait_ge(s_var, n + 1)
                    act.activation(sq[:, :], p_m[:, :], ACT.Ln, bias=eps_t[:, :]).then_inc(s_ln, 1)
                    act.wait_ge(s_ln, n + 1)
                    act.activation(sq[:, :], sq[:, :], ACT.Exp, scale=-0.5).then_inc(s_rs, 1)
                elif name == "in_x":
                    wait(act, s_conv, 2 * n)
                    if isinstance(n, int) and n == 0:
                        act.wait_ge(s_zero, 1)
                    else:
                        act.activation(xcv[:, :, 0:HALO], xcv[:, :, T:T + HALO], ACT.Copy).then_inc(s_halo, 1)
                        act.wait_ge(s_halo, n)
                    wait(act, s_dtu, n)
                    for g, bank in ((0, p_m), (1, p_two)):
                        act.wait_ge(s_xc, G * n + g + 1)
                        act.activation(xcv[:, g, HALO:HALO + T], bank[:, :], ACT.Copy)
                        act.activation(u[:, g, :], bank[:, :], ACT.Identity, bias=conv_b[:, g:g + 1],
                                       scale=conv_w[:, g, HALO:KC]).then_inc(s_xcv, 1)
                elif name in ("z0", "z1"):
                    g = int(name[1])
                    wait(act, s_yg, n - 1)
                    act.wait_ge(s_z, G * n + g + 1)
                    act.activation(gate[:, b, g, :], p_m[:, :], ACT.Copy).then_inc(s_zcopy, 1)
                elif name == "silu":
                    act.wait_ge(s_zcopy, G * (n + 1))
                    act.activation(gate[:, b, :, :], gate[:, b, :, :], ACT.Silu).then_inc(s_gate, 1)
                    act.wait_ge(s_conv, 2 * n + 2)
                    act.activation(u[:, :, :], u[:, :, :], ACT.Silu).then_inc(s_u, 1)
                    act.preload_act_table_set(LOG_EXP)
                elif name == "x_proj":
                    act.wait_ge(s_dbcp, n + 1)
                    act.activation(dbc[:, :], p_m[:, :], ACT.Copy).then_inc(s_dbc, 1)
                    act.wait_ge(s_u, n + 1)
                    for g in range(G):
                        act.activation(y[:, b, g, :], u[:, g, :], ACT.Copy,
                                       scale=D_skip[:, g:g + 1]).then_inc(s_yinit, 1)
                elif name in ("dt0", "dt1"):
                    g = int(name[2])
                    wait(act, s_dt, n)
                    act.wait_ge(s_dtp, G * n + g + 1)
                    act.activation(sp[:, g, :], (p_m, p_two)[g][:, :], ACT.Abs,
                                   bias=b_dt[:, g:g + 1]).then_inc(s_abs, 1)
                    act.activation(dt_[:, b, g, :], (p_m, p_two)[g][:, :], ACT.Relu,
                                   bias=b_dt[:, g:g + 1]).then_inc(s_relu, 1)
                elif name == "softplus":
                    act.wait_ge(s_abs, 3 * n + 2)
                    act.activation(sp[:, :, :], sp[:, :, :], ACT.Exp, scale=-1.0).then_inc(s_abs, 1)
                    act.wait_ge(s_abs, 3 * n + 3)
                    act.activation(sp[:, :, :], sp[:, :, :], ACT.Ln, bias=1.0).then_inc(s_sp, 1)
                elif name == "rstd_x1":
                    act.wait_ge(s_stats, 2 * (n + 1))
                    act.activation(rstd[:, :], mv[:, :, 1], ACT.Ln, bias=eps_t[:, :]).then_inc(s_rv, 1)
                    act.wait_ge(s_rv, 2 * n + 1)
                    act.activation(rstd[:, :], rstd[:, :], ACT.Exp, scale=-0.5).then_inc(s_rv, 1)
                elif name in ("mlp0", "mlp1", "mlp2"):
                    l = int(name[3])
                    act.wait_ge(s_mm2, 4 * n + l + 1)
                    act.activation(mb[:, l % 2, :], p_m[:, :], ACT.Relu, bias=b2[:, l:l + 1],
                                   scale=scale2[:, :] if l == 0 else 1.0).then_inc(s_mr2, 1)

            act.preload_act_table_set(LOG_EXP)
            act.wait_ge(s_pack, 16)
            act.activation(A[:, :, :], w("A_log").rearrange("p (g s) -> p g s", g=G), ACT.Exp).then_inc(s_A, 1)
            act.wait_ge(s_A, 1)
            act.activation(A[:, :, :], A[:, :, :], ACT.Copy, scale=-1.0).then_inc(s_A, 1)
            act.wait_ge(s_scales, 1)
            for name in PRE:
                step(name, 0, 0)
            act.wait_ge(s_A, 2)

            def body(c, b):
                decay(c, b, 0)
                for unit in range(S):
                    for name, n, nb in steps(EARLY, unit, c, b):
                        step(name, n, nb)
                    if unit < S - 1:
                        decay(c, b, unit + 1)
                    save_state(c, unit)
                    for name, n, nb in steps(LATE, unit, c, b):
                        step(name, n, nb)

            chunks(act, body)
            step("rstd_x1", NC - 1, 1)
            for t in range(NC + 5):
                for l, dst in ((2, sq), (1, hc), (0, hr)):
                    k = t - 1 - l
                    if 0 <= k < NC:
                        act.wait_ge(s_l, fcount(k, l))
                        if l == 2:
                            wait(act, s_mg, k)
                        act.activation(dst[:, :], layer_bank(l)[:, :], ACT.Relu, bias=b1[:, l:l + 1],
                                       scale=scale1[:, :] if l == 0 else 1.0).then_inc(s_f, 1)
                k = t - 4
                if 0 <= k < NC:
                    act.wait_ge(s_fst, 2 * k + 2)
                    act.activation(rstd[:, :], mv[:, :, 1], ACT.Ln, bias=eps_t[:, :]).then_inc(s_fv, 1)
                    act.wait_ge(s_fv, 2 * k + 1)
                    act.activation(rstd[:, :], rstd[:, :], ACT.Exp, scale=-0.5).then_inc(s_fv, 1)

        @block.vector
        def _(dve):
            def unit_ops(c, b, unit):
                q = unit % 2
                if unit == 0:
                    dve.wait_ge(s_dtu, c + 1)
                wait(dve, s_state, S * c + unit - 1)
                dve.wait_ge(s_bb, S * c + unit + 1)
                dve.tensor_tensor(bh[:, q, :, :], both(p_B), dtu[:, b, :, :], ALU.mult).then_inc(s_bmul, 1)
                dve.wait_ge(s_bmul, S * c + unit + 1)
                for g in range(G):
                    dve.wait_ge(s_dA, G * (S * c + unit) + g + 1)
                    first = 0.0 if isinstance(c, int) and c == 0 else state[:, unit, g:g + 1]
                    dve.tensor_tensor_scan(bh[:, q, g, :], p_dA[g][:, :], bh[:, q, g, :], first,
                                           ALU.mult, ALU.add).then_inc(s_scan, 1)
                wait(dve, s_acc, S * c + unit - 1)
                dve.wait_ge(s_cb, S * c + unit + 1)
                dve.wait_ge(s_scan, G * (S * c + unit + 1))
                dve.tensor_tensor(prod[:, q, :, :], both(p_C), bh[:, q, :, :], ALU.mult).then_inc(s_cmul, 1)

            def conv(n, g):
                dve.wait_ge(s_xcv, G * n + g + 1)
                for k in range(KC - 1):
                    if k:
                        dve.wait_ge(s_tap, (KC - 2) * (G * n + g) + k)
                    dve.scalar_tensor_tensor(out=u[:, g, :], in0=xcv[:, g, k:k + T], scalar=conv_w[:, g, k:k + 1],
                                             in1=u[:, g, :], op0=ALU.mult, op1=ALU.add
                                             ).then_inc(s_tap if k < KC - 2 else s_conv, 1)

            def add_two(i, k, done):
                dve.wait_ge(s_blk_used, done)
                dve.tensor_tensor(acc2[:, T * k:T * (k + 1)], two_bank(i)[:, :], acc2[:, T * k:T * (k + 1)],
                                  ALU.add).then_inc(s_two_add, 1)

            def statistics(src, s_st, n):
                for t in range(JT):
                    last = dve.bn_stats(bn6[:, t, :], src[:, t, :])
                last.then_inc(s_st, 1)
                dve.wait_ge(s_st, 2 * n + 1)

            def aggregate(s_st):
                for t in range(JT):
                    last = dve.bn_aggr(mv[:, t, :], bn6[:, t, :])
                last.then_inc(s_st, 1)

            def normalise(src, dst, s_v, s_done, n):
                dve.wait_ge(s_v, 2 * n + 2)
                for t in range(JT):
                    last = dve.tensor_scalar(dst[:, t, :], src[:, t, :], mv[:, t, 0:1], rstd[:, t:t + 1],
                                             ALU.subtract, ALU.mult)
                last.then_inc(s_done, 1)

            def step(name, n, b):
                if name == "mean":
                    dve.wait_ge(s_mu, n + 1)
                    dve.tensor_tensor(hc[:, :], hr[:, :], p_m[:, :], ALU.subtract).then_inc(s_hc, 1)
                elif name == "var":
                    dve.wait_ge(s_rs, n + 1)
                    dve.scalar_tensor_tensor(out=hc[:, :], in0=hc[:, :], scalar=w("ln_g"), in1=sq[:, :],
                                             op0=ALU.mult, op1=ALU.mult).then_inc(s_hg, 1)
                    dve.wait_ge(s_hg, n + 1)
                    dve.tensor_scalar(hc[:, :], hc[:, :], w("ln_b"), None, ALU.add).then_inc(s_h, 1)
                elif name in ("conv0", "conv1"):
                    conv(n, int(name[4]))
                elif name == "x_proj":
                    dve.wait_ge(s_dbc, n + 1)
                    part = bc[:, b, :]
                    chain = [4 * n]

                    def link(ins):
                        ins.then_inc(s_part, 1)
                        chain[0] = chain[0] + 1
                        dve.wait_ge(s_part, chain[0])

                    link(dve.tensor_copy(part, dbc[:, :]))
                    link(dve.tensor_tensor(rest[:, :], dbc[:, :], part, ALU.subtract))
                    link(dve.tensor_copy(bc[64:128, b, :], rest[64:128, :]))
                    link(dve.tensor_tensor(rest[96:128, :], rest[96:128, :], bc[96:128, b, :], ALU.subtract))
                    dve.tensor_copy(bc[96:128, b, :], rest[96:128, :]).then_inc(s_split, 1)
                elif name == "dt_sum":
                    dve.wait_ge(s_sp, n + 1)
                    dve.wait_ge(s_relu, G * (n + 1))
                    dve.tensor_tensor(dt_[:, b, :, :], dt_[:, b, :, :], sp[:, :, :], ALU.add).then_inc(s_dt, 1)
                elif name == "out":
                    dve.wait_ge(s_o, n + 1)
                    dve.tensor_tensor(r[:, :, :], p_m4, xs[:, bass.ds(JT * n, JT), 0:D], ALU.add).then_inc(s_r, 1)
                    dve.wait_ge(s_r, n + 1)
                    statistics(r, s_stats, n)
                elif name == "rstd_x1":
                    aggregate(s_stats)
                elif name == "ln_x1":
                    dve.wait_ge(s_blk_used, started(n + 1))
                    normalise(r, x1[:, b, :, :], s_rv, s_x1, n)
                    dve.wait_ge(s_res0, n + 1)
                    dve.wait_ge(s_x1, n + 1)
                    tiles = resid[:, bass.ds(JT * n, JT), :]
                    dve.tensor_tensor(tiles, tiles, x1[:, b, :, :], ALU.add).then_inc(s_res, 1)
                elif name == "mlp3":
                    dve.wait_ge(s_mm2, 4 * n + 4)
                    dve.tensor_tensor(resid[:, bass.ds(JT * n, JT), :], p_m4,
                                      bm[:, :].rearrange("p (t n) -> p t n", t=1).to_broadcast([P, JT, D]),
                                      ALU.add).then_inc(s_res0, 1)

            dve.memset(eps_t[:, :], EPS)
            dve.wait_ge(s_consts_in, 48)
            dve.tensor_scalar(scale1[:, :], scale1[:, :], 1.0, 1.0, ALU.add, ALU.add)
            dve.tensor_scalar(scale2[:, :], scale2[:, :], 1.0, 1.0, ALU.add, ALU.add).then_inc(s_scales, 1)
            dve.wait_ge(s_two_add, 1)
            dve.wait_ge(s_pack, 16)
            for name in PRE:
                step(name, 0, 0)

            def body(c, b):
                for unit in range(S):
                    for name, n, nb in steps(EARLY, unit, c, b):
                        step(name, n, nb)
                    unit_ops(c, b, unit)
                    if unit in two_units(c):
                        add_two(two_of(c, unit), two_chunks(c, unit)[1], place(c, unit, 2)[2])
                    for name, n, nb in steps(LATE, unit, c, b):
                        step(name, n, nb)

            chunks(dve, body)
            for i in range(AFTER):
                if i == 2:
                    step("out", NC - 1, 1)
                    step("rstd_x1", NC - 1, 1)
                add_two((NC - 1) * NBLK - AFTER + i, NBLK - AFTER + i, AFTER_AT + i + 1)
                if i == 2:
                    step("ln_x1", NC - 1, 1)
            for t in range(NC + 6):
                if t < NC:
                    add_two((NC - 1) * NBLK + t, t, TAIL_AT + t + 1)
                k = t - 5
                if 0 <= k < NC:
                    if k >= 2:
                        dve.wait_ge(s_out[k % 2], 16 * (k // 2))
                    normalise(r, mb4(k % 2), s_fv, s_fin, k)
                k = t - 4
                if 0 <= k < NC:
                    wait(dve, s_fin, k)
                    dve.wait_ge(s_mg, k + 1)
                    dve.tensor_tensor(r[:, :, :], merge_bank(k), resid[:, JT * k:JT * (k + 1), :],
                                      ALU.add).then_inc(s_fr, 1)
                    dve.wait_ge(s_fr, k + 1)
                    statistics(r, s_fst, k)
                    aggregate(s_fst)

        @block.gpsimd
        def _(pool):
            def add_product(c, b, unit):
                if unit == 0:
                    pool.wait_ge(s_yinit, G * (c + 1))
                pool.wait_ge(s_cmul, S * c + unit + 1)
                wait(pool, s_acc, S * c + unit)
                pool.tensor_tensor(y[:, b, :, :], y[:, b, :, :], prod[:, unit % 2, :, :],
                                   ALU.add).then_inc(s_acc, 1)

            def step(name, n, b):
                if name == "dt_sum":
                    pool.wait_ge(s_dt, n + 1)
                    pool.wait_ge(s_u, n + 1)
                    pool.tensor_tensor(dtu[:, b, :, :], dt_[:, b, :, :], u[:, :, :], ALU.mult).then_inc(s_dtu, 1)
                elif name == "gate_y":
                    pool.wait_ge(s_acc, S * (n + 1))
                    pool.wait_ge(s_gate, n + 1)
                    pool.tensor_tensor(yg[:, :, :], y[:, b, :, :], gate[:, b, :, :], ALU.mult).then_inc(s_yg, 1)
                elif name == "ln_x1":
                    pool.wait_ge(s_o, n + 1)

            pool.memset(w_dt[:, :], 0.0)
            pool.memset(xcv[:, :, 0:HALO], 0.0)
            pool.memset(sel[:, :], 0.0)
            pool.memset(wx3[:, :, :], 0.0).then_inc(s_zero, 1)
            pool.memset(acc2[:, :], 0.0).then_inc(s_two_add, 1)
            pool.memset(mean_w[:, :], 1.0 / D).then_inc(s_mean_w, 1)
            pool.wait_ge(s_zero, 1)
            for q in range(1, 4):
                if q > 1:
                    pool.wait_ge(s_sel, q - 1)
                pool.affine_select(out=sel[:, :], in_=sel[:, :], compare_op=ALU.not_equal, fill=1.0,
                                   base=-2 * S * q, pattern=[[-1, 2 * S]], channel_multiplier=1).then_inc(s_sel, 1)
            pool.wait_ge(s_pack, 16)
            pool.tensor_copy(wx3[:, :, 0:R], w_xp[:, :, 0:R])
            for q in range(1, 4):
                last = pool.tensor_copy(wx3[:, :, 2 * S * q:2 * S * (q + 1)], w_xp[:, :, R:R + 2 * S])
            last.then_inc(s_wx3, 1)
            for name in PRE:
                step(name, 0, 0)

            def body(c, b):
                for unit in range(S):
                    for name, n, nb in steps(EARLY, unit, c, b):
                        step(name, n, nb)
                    add_product(c, b, unit)
                    for name, n, nb in steps(LATE, unit, c, b):
                        step(name, n, nb)

            chunks(pool, body)
            step("gate_y", NC - 1, 1)
            step("ln_x1", NC - 1, 1)


def kernel(**inputs):
    import numpy as np
    import concourse.bacc as bacc
    from concourse.bass_utils import run_bass_kernel_spmd as run

    a = {k.replace("L0_gnn_", "").replace("L1_gnn_", ""): np.asarray(v) for k, v in inputs.items()}

    def rows(m):
        m = m.reshape(m.shape[0], -1)
        return m.reshape(-1, P, m.shape[1]).transpose(1, 0, 2).reshape(P, -1)

    parts = {
        "gcn_w": a["gcn_w"], "w_in": a["w_in"], "w_xp": rows(a["w_xp"]), "w_out": rows(a["w_out"]),
        "W1": a["W1"].transpose(2, 0, 1).reshape(D, -1), "W2": a["W2"].transpose(2, 0, 1).reshape(D, -1),
        "Wm": rows(a["Wm"].T), "gcn_b": rows(a["gcn_b"]), "ln_g": rows(a["ln_g"]), "ln_b": rows(a["ln_b"]),
        "conv_w": rows(a["conv_w"]), "conv_b": rows(a["conv_b"]), "b_dt": rows(a["b_dt"]),
        "D_skip": rows(a["D_skip"]), "A_log": rows(a["A_log"]), "b1": a["b1"].T, "b2": a["b2"].T,
    }
    adj = a["adj"].reshape(NC, T, NBLK, JT, P).transpose(0, 2, 4, 3, 1)
    xs = np.concatenate([a["x"], a["x2"]], axis=1).reshape(NC, JT, P, 2 * D).transpose(0, 2, 1, 3)
    arrays = {
        "adj_blocks": np.ascontiguousarray(adj),
        "xs_tiles": np.ascontiguousarray(xs),
        "pack_w": np.ascontiguousarray(np.concatenate([parts[n] for n in PACK], axis=1)),
        "w_dt_rows": np.ascontiguousarray(a["w_dt"]),
        "eps1_in": np.ascontiguousarray(a["eps1"]), "eps2_in": np.ascontiguousarray(a["eps2"]),
        "bm_in": np.ascontiguousarray(a["bm"]),
    }
    nc = bacc.Bacc("TRN2", target_bir_lowering=False, num_devices=1)
    d = {k: nc.dram_tensor(k, v.shape, F32, kind="ExternalInput").ap() for k, v in arrays.items()}
    out = nc.dram_tensor("out_tiles", (NC, P, JT, D), F32, kind="ExternalOutput").ap()

    def spread(ap):
        return ap.rearrange("(a n) -> a n", a=1).to_broadcast([P, ap.shape[0]])

    two_layer_graph_kernel(nc, d["adj_blocks"], d["xs_tiles"], d["pack_w"], d["w_dt_rows"],
                           spread(d["eps1_in"]), spread(d["eps2_in"]), spread(d["bm_in"]), out)
    res = run(nc, [arrays], core_ids=[0])
    got = res.results[0]["out_tiles"]
    return np.ascontiguousarray(got.transpose(0, 2, 1, 3).reshape(N, D))
```

```python
import concourse.bass as bass
from concourse import mybir
from contextlib import ExitStack

F32 = mybir.dt.float32
BF16 = mybir.dt.bfloat16
ALU = mybir.AluOpType
ACT = mybir.ActivationFunctionType

P = 128
N = 4096
D = 128
T = 512
NC = N // T
JT = T // P
G = 2
S = 16
R = 8
KC = 4
HALO = KC - 1
L = 3
NBLK = N // T
RING = 4
EPS = 1e-5
LOG_EXP = "natural_log_exp_and_others"

PACK = {}
_at = 0
for _n, _w in (("gcn_w", D), ("w_in", 4 * P), ("w_xp", G * (R + 2 * S)), ("w_out", G * D),
               ("W1", L * D), ("W2", L * D), ("Wm", 2 * D),
               ("gcn_b", 1), ("ln_g", 1), ("ln_b", 1), ("conv_w", G * KC), ("conv_b", G),
               ("b_dt", G), ("D_skip", G), ("A_log", G * S), ("b1", L), ("b2", L)):
    PACK[_n] = (_at, _at + _w)
    _at += _w
PACK_W = _at


def two_layer_graph_kernel(nc, blocks, xs_d, pack_d, w_dt_d, eps1_d, eps2_d, bm_d, out_d):
    ctx = ExitStack()
    with ctx:
        def sb(name, shape, dt=F32):
            return ctx.enter_context(nc.sbuf_tensor(name, shape, dt))

        def pb(name, shape=(P, T)):
            return ctx.enter_context(nc.psum_tensor(name, list(shape), F32))

        def sem(name):
            return ctx.enter_context(nc.semaphore(name))

        xs = sb("xs", [P, N // P, 2 * D])
        ring = sb("ring", [P, RING, JT, T])
        acc2 = sb("acc2", [P, N])
        resid = sb("resid", [P, N // P, D])
        dt_ = sb("dt", [P, 2, G, T])
        dtu = sb("dtu", [P, 2, G, T])
        gate = sb("gate", [P, 2, G, T])
        y = sb("y", [P, 2, G, T])
        bh = sb("bh", [P, 2, G, T])
        prod = sb("prod", [P, 2, G, T])
        bc = sb("bc", [P, 2, T], BF16)
        state = sb("state", [P, S, G])
        xcv = sb("xcv", [P, G, HALO + T])
        ax = sb("ax", [P, T])
        ax2 = sb("ax2", [P, T])
        hr = sb("hr", [P, T])
        hc = sb("hc", [P, T])
        sq = sb("sq", [P, T])
        u = sb("u", [P, G, T])
        dbc = sb("dbc", [P, T])
        rest = sb("rest", [P, T])
        sp = sb("sp", [P, G, T])
        mb = sb("mb", [P, 2, T])
        yg = sb("yg", [P, G, T])
        r = sb("r", [P, JT, D])
        x1 = sb("x1", [P, 2, JT, D])
        bn6 = sb("bn6", [P, JT, 6])
        mv = sb("mv", [P, 2, JT, 2])
        rstd = sb("rstd", [P, 2, JT])
        pack = sb("pack", [P, PACK_W])
        wx3 = sb("wx3", [P, G, P])
        w_dt = sb("w_dt", [P, G * P])
        A = sb("A", [P, G, S])
        mean_w = sb("mean_w", [P, P])
        sel = sb("sel", [P, 2 * S], BF16)
        bm = sb("bm", [P, D])
        scale1 = sb("scale1", [P, 1])
        scale2 = sb("scale2", [P, 1])
        eps_t = sb("eps_t", [P, 1])

        def w(name):
            return pack[:, PACK[name][0]:PACK[name][1]]

        gcn_w, w_in = w("gcn_w"), w("w_in")
        w_xp = w("w_xp").rearrange("p (g n) -> p g n", g=G)
        w_out = w("w_out").rearrange("p (g n) -> p g n", g=G)
        W1 = w("W1").rearrange("p (l n) -> p l n", l=L)
        W2 = w("W2").rearrange("p (l n) -> p l n", l=L)
        Wm = w("Wm").rearrange("p (b n) -> p b n", b=2)
        conv_w = w("conv_w").rearrange("p (g k) -> p g k", g=G)
        conv_b, b_dt, D_skip, b1, b2 = w("conv_b"), w("b_dt"), w("D_skip"), w("b1"), w("b2")

        p_x = pb("p_x")
        p_x2 = pb("p_x2")
        p_two = pb("p_two")
        p_dA = [pb("p_dA0"), pb("p_dA1")]
        p_B = pb("p_B")
        p_C = pb("p_C")
        p_m = pb("p_m")
        p_m4 = p_m[:, :].rearrange("p (t n) -> p t n", t=JT)

        def both(bank):
            return bank[:, :].rearrange("p (g t) -> p g t", g=1).to_broadcast([P, G, T])

        s_pack, s_wdt, s_consts_in = sem("s_pack"), sem("s_wdt"), sem("s_consts_in")
        s_xs = [sem(f"s_xs{i}") for i in range(NBLK)]
        s_zero, s_sel, s_A = sem("s_zero"), sem("s_sel"), sem("s_A")
        s_mean_w, s_wx3, s_scales, s_tap, s_part = (sem(n) for n in (
            "s_mean_w", "s_wx3", "s_scales", "s_tap", "s_part"))
        s_tile = [sem(f"s_tile{i}") for i in range(JT)]
        s_blk = [sem(f"s_blk{i}") for i in range(RING)]
        s_blk_used = sem("s_blk_used")
        s_bb, s_cb, s_dA = sem("s_bb"), sem("s_cb"), sem("s_dA")
        s_bmul, s_scan, s_cmul = sem("s_bmul"), sem("s_scan"), sem("s_cmul")
        s_state, s_acc = sem("s_state"), sem("s_acc")
        s_px, s_ax, s_ax2, s_gcn, s_hr = (sem(n) for n in ("s_px", "s_ax", "s_ax2", "s_gcn", "s_hr"))
        s_mu, s_hc, s_sq, s_var, s_ln, s_rs = (sem(n) for n in ("s_mu", "s_hc", "s_sq", "s_var", "s_ln", "s_rs"))
        s_hg, s_h, s_xc, s_halo, s_xcv, s_zcopy = (sem(n) for n in (
            "s_hg", "s_h", "s_xc", "s_halo", "s_xcv", "s_zcopy"))
        s_z, s_gate, s_conv, s_u, s_dbcp, s_dbc = (sem(n) for n in ("s_z", "s_gate", "s_conv", "s_u", "s_dbcp", "s_dbc"))
        s_yinit, s_split, s_dtp, s_abs, s_sp = (sem(n) for n in ("s_yinit", "s_split", "s_dtp", "s_abs", "s_sp"))
        s_relu, s_dt, s_dtu = (sem(n) for n in ("s_relu", "s_dt", "s_dtu"))
        s_yg, s_o, s_r, s_stats, s_rv, s_x1 = (sem(n) for n in ("s_yg", "s_o", "s_r", "s_stats", "s_rv", "s_x1"))
        s_mm2, s_mr2, s_res0, s_two_add = (sem(n) for n in ("s_mm2", "s_mr2", "s_res0", "s_two_add"))
        s_l, s_f, s_mg, s_fr, s_fst, s_fv, s_fin = (sem(n) for n in (
            "s_l", "s_f", "s_mg", "s_fr", "s_fst", "s_fv", "s_fin"))
        s_out = [sem("s_out0"), sem("s_out1")]

        def wait(eng, s, value):
            if isinstance(value, int) and value <= 0:
                return
            assert isinstance(value, int) or value.min_val > 0
            eng.wait_ge(s, value)

        EARLY = {0: ["gate_y"], 7: ["take_ax"], 8: ["gcn"], 11: ["z0"], 12: ["silu"], 13: ["x_proj"],
                 14: ["dt1", "softplus", "dtu"]}
        LATE = {1: ["out"], 2: ["rstd_x1"], 3: ["ln_x1", "mlp0"], 4: ["mlp1"], 5: ["mlp2"], 6: ["mlp3"],
                7: ["take_ax2"], 8: ["mean"], 9: ["var"], 10: ["in_x", "conv0"], 11: ["z1", "conv1"],
                13: ["dt0", "split"], 14: ["dt_sum"]}
        EARLY_LIGHT = {**EARLY, 14: ["softplus", "dtu"]}
        LATE_LIGHT = {**LATE, 1: [], 2: ["out"], 3: ["rstd_x1"], 4: ["ln_x1", "mlp0"], 5: ["mlp1"],
                      6: ["mlp2"], 7: ["take_ax2", "mlp3"], 13: ["dt0", "split", "dt1"]}
        POST = ("gate_y", "out", "rstd_x1", "ln_x1")
        MLP = ("mlp0", "mlp1", "mlp2", "mlp3")
        PRE = ("take_ax", "take_ax2", "gcn", "mean", "var", "in_x", "z0", "z1", "conv0", "conv1", "silu",
               "x_proj", "split", "dt0", "dt1", "softplus", "dt_sum", "dtu")
        FILL = {"gcn": 1, "mean": 1, "var": 3, "z1": 4, "x_proj": 1, "dt1": 6}

        def last_chunk(c, n):
            return isinstance(c, int) and c >= NC - n

        def steps(table, unit, c, b):
            if isinstance(c, int) and (c < 2 or c == NC - 2):
                table = EARLY_LIGHT if table is EARLY else LATE_LIGHT
            for name in table.get(unit, ()):
                if name in POST and not (isinstance(c, int) and c == 0):
                    yield name, c - 1, 1 - b
                elif name in MLP:
                    yield name, c, b
                elif name in PRE and not last_chunk(c, 1):
                    yield name, c + 1, 1 - b

        def two_units(c):
            if isinstance(c, int) and c < 2:
                return []
            if isinstance(c, int) and c == NC - 2:
                return list(range(S // 2, S))
            if isinstance(c, int) and c == NC - 1:
                return [0, 1] + list(range(4, S))
            return [1, 3, 5, 7, 9, 11, 13, 15]

        AFTER = 2

        def two_start(c):
            if isinstance(c, int) and c >= NC - 1:
                return two_start(c - 1) + len(two_units(c - 1))
            return (c - 2) * NBLK if not (isinstance(c, int) and c < 2) else 0

        def one_of(c, unit):
            if unit < S // 2:
                return None if last_chunk(c, 1) else (c + 1, NBLK // 2 + unit // 2)
            return None if last_chunk(c, 2) else (c + 2, (unit - S // 2) // 2)

        def two_of(c, unit):
            units = two_units(c)
            return two_start(c) + units.index(unit) if unit in units else None

        def two_chunks(c, unit):
            if isinstance(c, int):
                return two_block(two_of(c, unit))
            return c - 2, two_units(c).index(unit)

        LAST_TWO = two_start(NC - 1)
        LAST_BLOCKS = ([(NC - 3, k) for k in range(AFTER)]
                       + [(n, k) for k in range(AFTER, NBLK) for n in (NC - 3, NC - 2)]
                       + [(NC - 2, k) for k in range(AFTER)]
                       + [(NC - 1, k) for k in range(NBLK)])

        def two_block(i):
            return LAST_BLOCKS[i - LAST_TWO] if i >= LAST_TWO else (i // NBLK, i % NBLK)

        def opens(i):
            return not isinstance(i, int) or i <= LAST_TWO or two_block(i)[1] != two_block(i - 1)[1]

        def closes(i):
            return not isinstance(i, int) or i + 1 >= NC * NBLK or opens(i + 1)

        def sum_no(i):
            return sum(opens(j) for j in range(i + 1)) - 1 if isinstance(i, int) else i

        TURNS = two_start(NC - 2) + len([u_ for u_ in two_units(NC - 2) if u_ < S // 2])

        def two_bank(i):
            return (p_x, p_x2)[sum_no(i) % 2] if isinstance(i, int) and i >= TURNS else p_two

        def chunk_parity(c, b, unit):
            return two_chunks(c, unit)[0] % 2 if isinstance(c, int) else b

        def sequence(c):
            done = []
            for unit in range(S):
                if unit % 2 == 1 and one_of(c, unit) is not None:
                    done.append((unit, 1))
                if unit in two_units(c):
                    done.append((unit, 2))
            return done

        def started(c):
            if isinstance(c, int):
                return NBLK + NBLK // 2 + sum(len(sequence(k)) for k in range(c))
            return started(2) + 2 * NBLK * (c - 2)

        def place(c, unit, one_or_two):
            at = sequence(c).index((unit | 1 if one_or_two == 1 else unit, one_or_two))
            if isinstance(c, int):
                at = at + started(c)
                return at % RING, at // RING + (at % RING > 0), at + 1
            assert started(2) % RING == 0
            fill = started(2) // RING + (2 * NBLK // RING) * (c - 2) + at // RING + (at % RING > 0)
            return at % RING, fill, started(c) + at + 1

        def chunks(eng, body):
            body(0, 0)
            body(1, 1)
            with eng.Fori(2, NC - 3, 2) as c:
                body(c, 0)
                body(c + 1, 1)
            body(NC - 2, 0)
            body(NC - 1, 1)

        def mb4(k):
            return mb[:, k, :].rearrange("p (t n) -> p t n", t=JT)

        def last_r(k):
            return prod[:, k % 2, 0, :].rearrange("p (t n) -> p t n", t=JT)

        def fcount(k, l):
            done = 0
            for t in range(NC + 5):
                for ll in (2, 1, 0):
                    kk = t - 1 - ll
                    if 0 <= kk < NC:
                        done += 1
                        if (kk, ll) == (k, l):
                            return done
            return 0

        def layer_bank(l):
            return (p_dA[0], p_dA[1], p_B)[l]

        def merge_bank(k):
            return (p_C, p_m)[k % 2][:, :].rearrange("p (t n) -> p t n", t=JT)

        def one_done(n):
            if isinstance(n, int) and n == 0:
                return NBLK
            return place(n - 1, S // 2 - 1, 1)[2]

        AFTER_AT = started(NC)
        TAIL_AT = AFTER_AT + AFTER
        assert two_start(NC) + AFTER == (NC - 1) * NBLK

        block = ctx.enter_context(nc.Block())

        @block.sync
        def _(sp_):
            def load(at, used, rows, cols):
                wait(sp_, s_blk_used, used)
                sp_.dma_start(ring[:, at, :, :], blocks[rows, cols]).then_inc(s_blk[at], 16)

            for k in range(NBLK):
                if k == 0:
                    for jt in range(JT):
                        sp_.dma_start(xs[:, jt, :], xs_d[0, :, jt]).then_inc(s_tile[jt], 16)
                        sp_.dma_start(ring[:, 0, jt, :], blocks[0, 0, :, jt]).then_inc(s_tile[jt], 16)
                    continue
                sp_.dma_start(xs[:, JT * k:JT * (k + 1), :], xs_d[k]).then_inc(s_xs[k], 16)
                load(k % RING, k - RING + 1, 0, k)
                if k == 1:
                    sp_.dma_start(pack[:, :], pack_d).then_inc(s_pack, 16)
                if k == 3:
                    sp_.wait_ge(s_zero, 1)
                    sp_.dma_start(w_dt[0:R, :], w_dt_d).then_inc(s_wdt, 16)
                    sp_.dma_start(scale1[:, :], eps1_d).then_inc(s_consts_in, 16)
                    sp_.dma_start(scale2[:, :], eps2_d).then_inc(s_consts_in, 16)
                    sp_.dma_start(bm[:, :], bm_d).then_inc(s_consts_in, 16)
            for k in range(NBLK // 2):
                load(k % RING, NBLK + k - RING + 1, 1, k)

            def body(c, b):
                for unit, which in sequence(c):
                    slot, fill, done = place(c, unit, which)
                    if which == 1:
                        load(slot, done - RING, *one_of(c, unit))
                    else:
                        n, k = two_chunks(c, unit)
                        load(slot, done - RING, k, n)

            chunks(sp_, body)
            for i in range(AFTER):
                load((AFTER_AT + i) % RING, AFTER_AT + i - RING + 1, i, NC - 2)
            for k in range(NBLK):
                load((TAIL_AT + k) % RING, TAIL_AT + k - RING + 1, k, NC - 1)
            for k in range(NC):
                sp_.wait_ge(s_fin, k + 1)
                sp_.dma_start(out_d[k], mb4(k % 2)).then_inc(s_out[k % 2], 16)
            for q in range(2):
                sp_.wait_ge(s_out[q], 16 * (NC // 2))

        @block.tensor
        def _(pe):
            def broadcast_B(c, b, unit):
                if unit == 0:
                    pe.wait_ge(s_split, c + 1)
                wait(pe, s_bmul, S * c + unit)
                pe.matmul(p_B[:, :], sel[:, unit:unit + 1].to_broadcast([P, P]), bc[:, b, :],
                          start=True, stop=True).then_inc(s_bb, 1)

            def broadcast_C(c, b, unit):
                wait(pe, s_cmul, S * c + unit)
                pe.matmul(p_C[:, :], sel[:, S + unit:S + unit + 1].to_broadcast([P, P]), bc[:, b, :],
                          start=True, stop=True).then_inc(s_cb, 1)

            def one(n, k, tiles, slot, fill):
                if tiles[0] == 0:
                    wait(pe, s_blk[slot], 16 * fill)
                for bank, s_taken, half in ((p_x, s_ax, 0), (p_x2, s_ax2, 1)):
                    if k == 0 and tiles[0] == 0:
                        wait(pe, s_taken, n)
                    for jt in tiles:
                        j = JT * k + jt
                        last = pe.matmul(bank[:, :], xs[:, j, D * half:D * (half + 1)], ring[:, slot, jt, :],
                                         start=j == 0, stop=j == N // P - 1)
                    if half == 0 and j == N // P - 1:
                        last.then_inc(s_px, 1)
                if tiles[-1] == JT - 1:
                    last.then_inc(s_blk_used, 1)

            def two(i, n, b, k, slot, fill, tiles=range(JT)):
                if tiles[0] == 0:
                    if k == 0 or isinstance(i, int) and i >= LAST_TWO:
                        pe.wait_ge(s_x1, n + 1)
                    if not opens(i):
                        pass
                    elif isinstance(i, int) and i >= TURNS:
                        pe.wait_ge(s_two_add, sum_no(i))
                        if i < TURNS + 2:
                            pe.wait_ge((s_ax, s_ax2)[i % 2], NC)
                    else:
                        pe.wait_ge(s_two_add, i + 1)
                    pe.wait_ge(s_blk[slot], 16 * fill)
                for jt in tiles:
                    last = pe.matmul(two_bank(i)[:, :], x1[:, b, jt, :], ring[:, slot, jt, :],
                                     start=jt == 0 and opens(i), stop=jt == JT - 1 and closes(i))
                if tiles[-1] == JT - 1:
                    last.then_inc(s_blk_used, 1)

            def adjacency(c, b, unit):
                tiles = ()
                if one_of(c, unit) is not None:
                    slot, fill, _ = place(c, unit, 1)
                    cut = 3 if (unit | 1) in two_units(c) else 2
                    tiles = range(cut) if unit % 2 == 0 else range(cut, JT)
                    one(*one_of(c, unit), tiles[:1], slot, fill)
                if unit in two_units(c):
                    n, k = two_chunks(c, unit)
                    args = (two_of(c, unit), n, chunk_parity(c, b, unit), k, *place(c, unit, 2)[:2])
                    if not last_chunk(c, 2):
                        for q, s_read in ((10, s_xcv), (14, s_relu)):
                            if [u_ for u_ in two_units(c) if u_ > q][:1] == [unit]:
                                pe.wait_ge(s_read, G * (c + 2))
                    if unit == two_units(c)[0] and not last_chunk(c, 2):
                        pe.wait_ge(s_relu, G * (c + 1))
                    before_C = JT // 2 if not tiles else 1 if unit == 1 else 0
                    if before_C:
                        two(*args, range(before_C))
                for name, n, nb in steps(EARLY, unit, c, b):
                    step(name, n, nb)
                broadcast_C(c, b, unit)
                if 0 < unit < S - 1:
                    broadcast_B(c, b, unit + 1)
                if tiles[1:]:
                    one(*one_of(c, unit), tiles[1:], slot, fill)
                if unit in two_units(c):
                    two(*args, range(before_C, JT))

            def two_is_added(c, unit):
                before = [u_ for u_ in two_units(c) if u_ < (unit if not last_chunk(c, 2) else S // 2)]
                wait(pe, s_two_add, two_start(c) + len(before) + 1)

            def step(name, n, b):
                if name == "gcn":
                    pe.wait_ge(s_ax, n + 1)
                    wait(pe, s_res0, n)
                    pe.matmul(p_m[:, :], gcn_w, ax[:, :], start=True, stop=True).then_inc(s_gcn, 1)
                elif name == "mean":
                    pe.wait_ge(s_hr, n + 1)
                    pe.matmul(p_m[:, :], mean_w[:, :], hr[:, :], start=True, stop=True).then_inc(s_mu, 1)
                elif name == "var":
                    pe.wait_ge(s_sq, n + 1)
                    pe.matmul(p_m[:, :], mean_w[:, :], sq[:, :], start=True, stop=True).then_inc(s_var, 1)
                elif name == "in_x":
                    pe.wait_ge(s_h, n + 1)
                    pe.matmul(p_m[:, :], w_in[:, 0:P], hc[:, :], start=True, stop=True).then_inc(s_xc, 1)
                    if not (isinstance(n, int) and n == 0):
                        two_is_added(n - 1, 10)
                    pe.matmul(p_two[:, :], w_in[:, P:2 * P], hc[:, :], start=True, stop=True).then_inc(s_xc, 1)
                elif name in ("z0", "z1"):
                    g = int(name[1])
                    if g == 0:
                        pe.wait_ge(s_xcv, G * n + 1)
                    else:
                        pe.wait_ge(s_zcopy, G * n + 1)
                    pe.matmul(p_m[:, :], w_in[:, P * (G + g):P * (G + g + 1)], hc[:, :],
                              start=True, stop=True).then_inc(s_z, 1)
                elif name == "x_proj":
                    pe.wait_ge(s_zcopy, G * (n + 1))
                    pe.wait_ge(s_u, n + 1)
                    for g in range(G):
                        last = pe.matmul(p_m[:, :], wx3[:, g, :], u[:, g, :], start=g == 0, stop=g == G - 1)
                    last.then_inc(s_dbcp, 1)
                elif name in ("dt0", "dt1"):
                    g = int(name[2])
                    if g == 0:
                        pe.wait_ge(s_dbc, n + 1)
                    elif not (isinstance(n, int) and n == 0):
                        two_is_added(n - 1, 14)
                    else:
                        pe.wait_ge(s_xcv, G)
                    pe.matmul((p_m, p_two)[g][:, :], w_dt[:, P * g:P * (g + 1)], dbc[:, :],
                              start=True, stop=True).then_inc(s_dtp, 1)
                elif name == "out":
                    pe.wait_ge(s_yg, n + 1)
                    if not (isinstance(n, int) and n == NC - 1):
                        pe.wait_ge(s_relu, G * (n + 1) + 1)
                    else:
                        pe.wait_ge(s_res0, NC)
                    for t in range(JT):
                        for g in range(G):
                            last = pe.matmul(p_m4[:, t, :], yg[:, g, P * t:P * (t + 1)], w_out[:, g, :],
                                             start=g == 0, stop=g == G - 1)
                    last.then_inc(s_o, 1)
                elif name == "mlp0":
                    pe.wait_ge(s_ax2, n + 1)
                    if isinstance(n, int) and n == 0:
                        pe.wait_ge(s_relu, 1)
                    else:
                        pe.wait_ge(s_r, n)
                    pe.matmul(p_m[:, :], W2[:, 0, :], ax2[:, :], start=True, stop=True).then_inc(s_mm2, 1)
                elif name in ("mlp1", "mlp2"):
                    l = int(name[3])
                    pe.wait_ge(s_mr2, L * n + l)
                    pe.matmul(p_m[:, :], W2[:, l, :], mb[:, (l - 1) % 2, :], start=True, stop=True).then_inc(s_mm2, 1)
                elif name == "mlp3":
                    pe.wait_ge(s_mr2, L * n + L)
                    for t in range(JT):
                        last = pe.matmul(p_m4[:, t, :], mb[:, 0, P * t:P * (t + 1)], Wm[:, 1, :],
                                         start=True, stop=True)
                    last.then_inc(s_mm2, 1)

            for jt in range(JT):
                pe.wait_ge(s_tile[jt], 32)
                one(0, 0, [jt], 0, 0)
            for k in range(1, NBLK):
                pe.wait_ge(s_xs[k], 16)
                one(0, k, range(JT), k % RING, k // RING + (k % RING > 0))
            pe.wait_ge(s_pack, 16)
            pe.wait_ge(s_wx3, 1)
            pe.wait_ge(s_mean_w, 1)
            pe.wait_ge(s_sel, 3)
            pe.wait_ge(s_wdt, 16)
            tile = 0
            for name in PRE:
                step(name, 0, 0)
                for _ in range(FILL.get(name, 0)):
                    k = tile // JT
                    one(1, k, [tile % JT], k % RING, (NBLK + k) // RING + (k % RING > 0))
                    tile += 1
            assert tile == JT * NBLK // 2

            def body(c, b):
                for unit in range(S):
                    if unit == 0:
                        broadcast_B(c, b, 0)
                    adjacency(c, b, unit)
                    if unit == 0:
                        broadcast_B(c, b, 1)
                    for name, n, nb in steps(LATE, unit, c, b):
                        step(name, n, nb)

            chunks(pe, body)

            def after(i):
                at = AFTER_AT + i
                two((NC - 1) * NBLK - AFTER + i, NC - 2, 0, i, at % RING, at // RING + (at % RING > 0))

            after(0)
            step("out", NC - 1, 1)
            after(1)

            for t in range(NC + 5):
                if t < NC:
                    two((NC - 1) * NBLK + t, NC - 1, 1, t, (TAIL_AT + t) % RING,
                        (TAIL_AT + t) // RING + ((TAIL_AT + t) % RING > 0))
                if 0 <= t - 4 < NC:
                    k = t - 4
                    pe.wait_ge(s_f, fcount(k, 2))
                    wait(pe, s_fr, k - 1)
                    for jt in range(JT):
                        last = pe.matmul(merge_bank(k)[:, jt, :], sq[:, P * jt:P * (jt + 1)], Wm[:, 0, :],
                                         start=True, stop=True)
                    last.then_inc(s_mg, 1)
                for l, src in ((2, hc), (1, hr), (0, None)):
                    k = t - 1 - l
                    if 0 <= k < NC:
                        if l:
                            pe.wait_ge(s_f, fcount(k, l - 1))
                            moving = src[:, :]
                        else:
                            pe.wait_ge(s_two_add, sum_no(NBLK * (NC - 1) + k) + 2)
                            wait(pe, s_f, fcount(k - 1, 0))
                            moving = acc2[:, T * k:T * (k + 1)]
                        pe.matmul(layer_bank(l)[:, :], W1[:, l, :], moving, start=True, stop=True).then_inc(s_l, 1)

        @block.scalar
        def _(act):
            def decay(c, b, unit):
                if unit == 0:
                    act.wait_ge(s_dt, c + 1)
                for g in range(G):
                    wait(act, s_scan, G * (S * c + unit - 1) + g + 1)
                    act.activation(p_dA[g][:, :], dt_[:, b, g, :], ACT.Exp,
                                   scale=A[:, g, unit:unit + 1]).then_inc(s_dA, 1)

            def save_state(c, unit):
                act.wait_ge(s_scan, G * (S * c + unit + 1))
                act.activation(state[:, unit, :], bh[:, unit % 2, :, T - 1], ACT.Copy).then_inc(s_state, 1)

            def step(name, n, b):
                if name == "take_ax":
                    act.wait_ge(s_px, n + 1)
                    wait(act, s_gcn, n)
                    act.activation(ax[:, :], p_x[:, :], ACT.Copy).then_inc(s_ax, 1)
                elif name == "take_ax2":
                    act.wait_ge(s_blk_used, one_done(n))
                    wait(act, s_mm2, 4 * (n - 1) + 1)
                    act.activation(ax2[:, :], p_x2[:, :], ACT.Copy).then_inc(s_ax2, 1)
                elif name == "gcn":
                    act.wait_ge(s_gcn, n + 1)
                    act.activation(hr[:, :], p_m[:, :], ACT.Relu, bias=w("gcn_b")).then_inc(s_hr, 1)
                elif name == "mean":
                    act.wait_ge(s_hc, n + 1)
                    act.activation(sq[:, :], hc[:, :], ACT.Square).then_inc(s_sq, 1)
                elif name == "var":
                    act.wait_ge(s_var, n + 1)
                    act.activation(sq[:, :], p_m[:, :], ACT.Ln, bias=eps_t[:, :]).then_inc(s_ln, 1)
                    act.wait_ge(s_ln, n + 1)
                    act.activation(sq[:, :], sq[:, :], ACT.Exp, scale=-0.5).then_inc(s_rs, 1)
                elif name == "in_x":
                    wait(act, s_conv, 2 * n)
                    if isinstance(n, int) and n == 0:
                        act.wait_ge(s_zero, 1)
                    else:
                        act.activation(xcv[:, :, 0:HALO], xcv[:, :, T:T + HALO], ACT.Copy).then_inc(s_halo, 1)
                        act.wait_ge(s_halo, n)
                    wait(act, s_dtu, n)
                    for g, bank in ((0, p_m), (1, p_two)):
                        act.wait_ge(s_xc, G * n + g + 1)
                        act.activation(xcv[:, g, HALO:HALO + T], bank[:, :], ACT.Copy)
                        act.activation(u[:, g, :], bank[:, :], ACT.Identity, bias=conv_b[:, g:g + 1],
                                       scale=conv_w[:, g, HALO:KC]).then_inc(s_xcv, 1)
                elif name in ("z0", "z1"):
                    g = int(name[1])
                    wait(act, s_yg, n - 1)
                    act.wait_ge(s_z, G * n + g + 1)
                    act.activation(gate[:, b, g, :], p_m[:, :], ACT.Copy).then_inc(s_zcopy, 1)
                elif name == "silu":
                    act.wait_ge(s_conv, 2 * n + 2)
                    act.activation(u[:, :, :], u[:, :, :], ACT.Silu).then_inc(s_u, 1)
                    act.wait_ge(s_zcopy, G * (n + 1))
                    act.activation(gate[:, b, :, :], gate[:, b, :, :], ACT.Silu).then_inc(s_gate, 1)
                    act.preload_act_table_set(LOG_EXP)
                elif name == "x_proj":
                    act.wait_ge(s_dbcp, n + 1)
                    act.activation(dbc[:, :], p_m[:, :], ACT.Copy).then_inc(s_dbc, 1)
                    act.wait_ge(s_u, n + 1)
                    for g in range(G):
                        act.activation(y[:, b, g, :], u[:, g, :], ACT.Copy,
                                       scale=D_skip[:, g:g + 1]).then_inc(s_yinit, 1)
                elif name in ("dt0", "dt1"):
                    g = int(name[2])
                    wait(act, s_dt, n)
                    act.wait_ge(s_dtp, G * n + g + 1)
                    act.activation(sp[:, g, :], (p_m, p_two)[g][:, :], ACT.Abs,
                                   bias=b_dt[:, g:g + 1]).then_inc(s_abs, 1)
                    act.activation(dt_[:, b, g, :], (p_m, p_two)[g][:, :], ACT.Relu,
                                   bias=b_dt[:, g:g + 1]).then_inc(s_relu, 1)
                elif name == "softplus":
                    act.wait_ge(s_abs, 3 * n + 2)
                    act.activation(sp[:, :, :], sp[:, :, :], ACT.Exp, scale=-1.0).then_inc(s_abs, 1)
                    act.wait_ge(s_abs, 3 * n + 3)
                    act.activation(sp[:, :, :], sp[:, :, :], ACT.Ln, bias=1.0).then_inc(s_sp, 1)
                elif name == "rstd_x1":
                    act.wait_ge(s_stats, 2 * (n + 1))
                    act.activation(rstd[:, b, :], mv[:, b, :, 1], ACT.Ln, bias=eps_t[:, :]).then_inc(s_rv, 1)
                    act.wait_ge(s_rv, 2 * n + 1)
                    act.activation(rstd[:, b, :], rstd[:, b, :], ACT.Exp, scale=-0.5).then_inc(s_rv, 1)
                elif name in ("mlp0", "mlp1", "mlp2"):
                    l = int(name[3])
                    act.wait_ge(s_mm2, 4 * n + l + 1)
                    act.activation(mb[:, l % 2, :], p_m[:, :], ACT.Relu, bias=b2[:, l:l + 1],
                                   scale=scale2[:, :] if l == 0 else 1.0).then_inc(s_mr2, 1)

            act.preload_act_table_set(LOG_EXP)
            act.wait_ge(s_pack, 16)
            act.activation(A[:, :, :], w("A_log").rearrange("p (g s) -> p g s", g=G), ACT.Exp).then_inc(s_A, 1)
            act.wait_ge(s_A, 1)
            act.activation(A[:, :, :], A[:, :, :], ACT.Copy, scale=-1.0).then_inc(s_A, 1)
            act.wait_ge(s_scales, 1)
            for name in PRE:
                step(name, 0, 0)
            act.wait_ge(s_A, 2)

            def body(c, b):
                decay(c, b, 0)
                for unit in range(S):
                    for name, n, nb in steps(EARLY, unit, c, b):
                        step(name, n, nb)
                    if unit < S - 1:
                        decay(c, b, unit + 1)
                    save_state(c, unit)
                    for name, n, nb in steps(LATE, unit, c, b):
                        step(name, n, nb)

            chunks(act, body)
            step("rstd_x1", NC - 1, 1)
            for t in range(NC + 5):
                for l, dst in ((2, sq), (1, hc), (0, hr)):
                    k = t - 1 - l
                    if 0 <= k < NC:
                        act.wait_ge(s_l, fcount(k, l))
                        if l == 2:
                            wait(act, s_mg, k)
                        act.activation(dst[:, :], layer_bank(l)[:, :], ACT.Relu, bias=b1[:, l:l + 1],
                                       scale=scale1[:, :] if l == 0 else 1.0).then_inc(s_f, 1)
                k = t - 4
                if 0 <= k < NC:
                    b = k % 2
                    act.wait_ge(s_fst, 2 * k + 2)
                    act.activation(rstd[:, b, :], mv[:, b, :, 1], ACT.Ln, bias=eps_t[:, :]).then_inc(s_fv, 1)
                    act.wait_ge(s_fv, 2 * k + 1)
                    act.activation(rstd[:, b, :], rstd[:, b, :], ACT.Exp, scale=-0.5).then_inc(s_fv, 1)

        @block.vector
        def _(dve):
            def times_B(c, b, unit):
                wait(dve, s_state, S * c + unit - 1)
                wait(dve, s_cmul, S * c + unit - 1)
                dve.wait_ge(s_bb, S * c + unit + 1)
                dve.tensor_tensor(bh[:, unit % 2, :, :], both(p_B), dtu[:, b, :, :], ALU.mult).then_inc(s_bmul, 1)

            def unit_ops(c, b, unit):
                q = unit % 2
                if unit == 0:
                    dve.wait_ge(s_dtu, c + 1)
                    times_B(c, b, 0)
                dve.wait_ge(s_bmul, S * c + unit + 1)
                for g in range(G):
                    dve.wait_ge(s_dA, G * (S * c + unit) + g + 1)
                    first = 0.0 if isinstance(c, int) and c == 0 else state[:, unit, g:g + 1]
                    dve.tensor_tensor_scan(bh[:, q, g, :], p_dA[g][:, :], bh[:, q, g, :], first,
                                           ALU.mult, ALU.add).then_inc(s_scan, 1)
                if unit < S - 1:
                    times_B(c, b, unit + 1)
                wait(dve, s_acc, S * c + unit - 1)
                dve.wait_ge(s_cb, S * c + unit + 1)
                dve.wait_ge(s_scan, G * (S * c + unit + 1))
                dve.tensor_tensor(prod[:, q, :, :], both(p_C), bh[:, q, :, :], ALU.mult).then_inc(s_cmul, 1)

            def conv(n, g):
                dve.wait_ge(s_xcv, G * n + g + 1)
                for k in range(KC - 1):
                    if k:
                        dve.wait_ge(s_tap, (KC - 2) * (G * n + g) + k)
                    dve.scalar_tensor_tensor(out=u[:, g, :], in0=xcv[:, g, k:k + T], scalar=conv_w[:, g, k:k + 1],
                                             in1=u[:, g, :], op0=ALU.mult, op1=ALU.add
                                             ).then_inc(s_tap if k < KC - 2 else s_conv, 1)

            def add_two(i, k, done):
                if not closes(i):
                    return
                dve.wait_ge(s_blk_used, done)
                dve.tensor_tensor(acc2[:, T * k:T * (k + 1)], two_bank(i)[:, :], acc2[:, T * k:T * (k + 1)],
                                  ALU.add).then_inc(s_two_add, 1)

            def statistics(src, s_st, n):
                for t in range(JT):
                    last = dve.bn_stats(bn6[:, t, :], src[:, t, :])
                last.then_inc(s_st, 1)
                dve.wait_ge(s_st, 2 * n + 1)

            def aggregate(s_st, b):
                for t in range(JT):
                    last = dve.bn_aggr(mv[:, b, t, :], bn6[:, t, :])
                last.then_inc(s_st, 1)

            def normalise(src, dst, s_v, s_done, n, b):
                dve.wait_ge(s_v, 2 * n + 2)
                for t in range(JT):
                    last = dve.tensor_scalar(dst[:, t, :], src[:, t, :], mv[:, b, t, 0:1], rstd[:, b, t:t + 1],
                                             ALU.subtract, ALU.mult)
                last.then_inc(s_done, 1)

            def step(name, n, b):
                if name == "mean":
                    dve.wait_ge(s_mu, n + 1)
                    dve.tensor_tensor(hc[:, :], hr[:, :], p_m[:, :], ALU.subtract).then_inc(s_hc, 1)
                elif name == "var":
                    dve.wait_ge(s_rs, n + 1)
                    dve.scalar_tensor_tensor(out=hc[:, :], in0=hc[:, :], scalar=w("ln_g"), in1=sq[:, :],
                                             op0=ALU.mult, op1=ALU.mult).then_inc(s_hg, 1)
                    dve.wait_ge(s_hg, n + 1)
                    dve.tensor_scalar(hc[:, :], hc[:, :], w("ln_b"), None, ALU.add).then_inc(s_h, 1)
                elif name in ("conv0", "conv1"):
                    conv(n, int(name[4]))
                elif name == "split":
                    dve.wait_ge(s_dbc, n + 1)
                    part = bc[:, b, :]
                    chain = [4 * n]

                    def link(ins):
                        ins.then_inc(s_part, 1)
                        chain[0] = chain[0] + 1
                        dve.wait_ge(s_part, chain[0])

                    link(dve.tensor_copy(part, dbc[:, :]))
                    link(dve.tensor_tensor(rest[:, :], dbc[:, :], part, ALU.subtract))
                    link(dve.tensor_copy(bc[64:128, b, :], rest[64:128, :]))
                    link(dve.tensor_tensor(rest[96:128, :], rest[96:128, :], bc[96:128, b, :], ALU.subtract))
                    dve.tensor_copy(bc[96:128, b, :], rest[96:128, :]).then_inc(s_split, 1)
                elif name == "dt_sum":
                    dve.wait_ge(s_sp, n + 1)
                    dve.wait_ge(s_relu, G * (n + 1))
                    dve.tensor_tensor(dt_[:, b, :, :], dt_[:, b, :, :], sp[:, :, :], ALU.add).then_inc(s_dt, 1)
                elif name == "out":
                    dve.wait_ge(s_o, n + 1)
                    dve.tensor_tensor(r[:, :, :], p_m4, xs[:, bass.ds(JT * n, JT), 0:D], ALU.add).then_inc(s_r, 1)
                    dve.wait_ge(s_r, n + 1)
                    statistics(r, s_stats, n)
                elif name == "rstd_x1":
                    aggregate(s_stats, b)
                elif name == "ln_x1":
                    dve.wait_ge(s_blk_used, started(n + 1))
                    normalise(r, x1[:, b, :, :], s_rv, s_x1, n, b)
                    dve.wait_ge(s_res0, n + 1)
                    dve.wait_ge(s_x1, n + 1)
                    tiles = resid[:, bass.ds(JT * n, JT), :]
                    dve.tensor_tensor(tiles, tiles, x1[:, b, :, :], ALU.add)
                elif name == "mlp3":
                    dve.wait_ge(s_mm2, 4 * n + 4)
                    dve.tensor_tensor(resid[:, bass.ds(JT * n, JT), :], p_m4,
                                      bm[:, :].rearrange("p (t n) -> p t n", t=1).to_broadcast([P, JT, D]),
                                      ALU.add).then_inc(s_res0, 1)

            dve.memset(eps_t[:, :], EPS)
            dve.wait_ge(s_consts_in, 48)
            dve.tensor_scalar(scale1[:, :], scale1[:, :], 1.0, 1.0, ALU.add, ALU.add)
            dve.tensor_scalar(scale2[:, :], scale2[:, :], 1.0, 1.0, ALU.add, ALU.add).then_inc(s_scales, 1)
            dve.wait_ge(s_two_add, 1)
            dve.wait_ge(s_pack, 16)
            for name in PRE:
                step(name, 0, 0)

            def body(c, b):
                for unit in range(S):
                    for name, n, nb in steps(EARLY, unit, c, b):
                        step(name, n, nb)
                    unit_ops(c, b, unit)
                    if unit in two_units(c):
                        add_two(two_of(c, unit), two_chunks(c, unit)[1], place(c, unit, 2)[2])
                    for name, n, nb in steps(LATE, unit, c, b):
                        step(name, n, nb)

            chunks(dve, body)
            dve.wait_ge(s_cmul, S * NC)
            dve.wait_ge(s_acc, S * NC - 1)
            dve.tensor_tensor(y[:, 1, :, :], y[:, 1, :, :], prod[:, 1, :, :], ALU.add).then_inc(s_acc, 1)
            dve.wait_ge(s_acc, S * NC)
            dve.wait_ge(s_gate, NC)
            dve.tensor_tensor(yg[:, :, :], y[:, 1, :, :], gate[:, 1, :, :], ALU.mult).then_inc(s_yg, 1)
            add_two((NC - 1) * NBLK - AFTER, 0, AFTER_AT + 1)
            step("out", NC - 1, 1)
            step("rstd_x1", NC - 1, 1)
            step("ln_x1", NC - 1, 1)
            add_two((NC - 1) * NBLK - AFTER + 1, 1, AFTER_AT + 2)
            for t in range(NC + 6):
                if t < NC:
                    add_two((NC - 1) * NBLK + t, t, TAIL_AT + t + 1)
                k = t - 4
                if 0 <= k < NC:
                    wait(dve, s_fin, k - 1)
                    dve.wait_ge(s_mg, k + 1)
                    dve.tensor_tensor(last_r(k), merge_bank(k), resid[:, JT * k:JT * (k + 1), :],
                                      ALU.add).then_inc(s_fr, 1)
                    dve.wait_ge(s_fr, k + 1)
                    statistics(last_r(k), s_fst, k)
                    aggregate(s_fst, k % 2)
                k = t - 5
                if 0 <= k < NC:
                    if k >= 2:
                        dve.wait_ge(s_out[k % 2], 16 * (k // 2))
                    normalise(last_r(k), mb4(k % 2), s_fv, s_fin, k, k % 2)

        @block.gpsimd
        def _(pool):
            def add_product(c, b, unit):
                if unit == 0:
                    pool.wait_ge(s_yinit, G * (c + 1))
                pool.wait_ge(s_cmul, S * c + unit + 1)
                wait(pool, s_acc, S * c + unit)
                pool.tensor_tensor(y[:, b, :, :], y[:, b, :, :], prod[:, unit % 2, :, :],
                                   ALU.add).then_inc(s_acc, 1)

            def step(name, n, b):
                if name == "dtu":
                    pool.wait_ge(s_dt, n + 1)
                    pool.wait_ge(s_u, n + 1)
                    pool.tensor_tensor(dtu[:, b, :, :], dt_[:, b, :, :], u[:, :, :], ALU.mult).then_inc(s_dtu, 1)
                elif name == "gate_y":
                    pool.wait_ge(s_acc, S * (n + 1))
                    pool.wait_ge(s_gate, n + 1)
                    pool.tensor_tensor(yg[:, :, :], y[:, b, :, :], gate[:, b, :, :], ALU.mult).then_inc(s_yg, 1)
                elif name == "ln_x1":
                    pool.wait_ge(s_o, n + 1)

            pool.memset(w_dt[:, :], 0.0)
            pool.memset(xcv[:, :, 0:HALO], 0.0)
            pool.memset(sel[:, :], 0.0)
            pool.memset(wx3[:, :, :], 0.0).then_inc(s_zero, 1)
            pool.memset(acc2[:, :], 0.0).then_inc(s_two_add, 1)
            pool.memset(mean_w[:, :], 1.0 / D).then_inc(s_mean_w, 1)
            pool.wait_ge(s_zero, 1)
            for q in range(1, 4):
                if q > 1:
                    pool.wait_ge(s_sel, q - 1)
                pool.affine_select(out=sel[:, :], in_=sel[:, :], compare_op=ALU.not_equal, fill=1.0,
                                   base=-2 * S * q, pattern=[[-1, 2 * S]], channel_multiplier=1).then_inc(s_sel, 1)
            pool.wait_ge(s_pack, 16)
            pool.tensor_copy(wx3[:, :, 0:R], w_xp[:, :, 0:R])
            for q in range(1, 4):
                last = pool.tensor_copy(wx3[:, :, 2 * S * q:2 * S * (q + 1)], w_xp[:, :, R:R + 2 * S])
            last.then_inc(s_wx3, 1)
            for name in PRE:
                step(name, 0, 0)

            def body(c, b):
                for unit in range(S):
                    for name, n, nb in steps(EARLY, unit, c, b):
                        step(name, n, nb)
                    if not (last_chunk(c, 1) and unit == S - 1):
                        add_product(c, b, unit)
                    for name, n, nb in steps(LATE, unit, c, b):
                        step(name, n, nb)

            chunks(pool, body)


def kernel(**inputs):
    import numpy as np
    import concourse.bacc as bacc
    from concourse.bass_utils import run_bass_kernel_spmd as run

    a = {k.replace("L0_gnn_", "").replace("L1_gnn_", ""): np.asarray(v) for k, v in inputs.items()}

    def rows(m):
        m = m.reshape(m.shape[0], -1)
        return m.reshape(-1, P, m.shape[1]).transpose(1, 0, 2).reshape(P, -1)

    parts = {
        "gcn_w": a["gcn_w"], "w_in": a["w_in"], "w_xp": rows(a["w_xp"]), "w_out": rows(a["w_out"]),
        "W1": a["W1"].transpose(2, 0, 1).reshape(D, -1), "W2": a["W2"].transpose(2, 0, 1).reshape(D, -1),
        "Wm": rows(a["Wm"].T), "gcn_b": rows(a["gcn_b"]), "ln_g": rows(a["ln_g"]), "ln_b": rows(a["ln_b"]),
        "conv_w": rows(a["conv_w"]), "conv_b": rows(a["conv_b"]), "b_dt": rows(a["b_dt"]),
        "D_skip": rows(a["D_skip"]), "A_log": rows(a["A_log"]), "b1": a["b1"].T, "b2": a["b2"].T,
    }
    adj = a["adj"].reshape(NC, T, NBLK, JT, P).transpose(0, 2, 4, 3, 1)
    xs = np.concatenate([a["x"], a["x2"]], axis=1).reshape(NC, JT, P, 2 * D).transpose(0, 2, 1, 3)
    arrays = {
        "adj_blocks": np.ascontiguousarray(adj),
        "xs_tiles": np.ascontiguousarray(xs),
        "pack_w": np.ascontiguousarray(np.concatenate([parts[n] for n in PACK], axis=1)),
        "w_dt_rows": np.ascontiguousarray(a["w_dt"]),
        "eps1_in": np.ascontiguousarray(a["eps1"]), "eps2_in": np.ascontiguousarray(a["eps2"]),
        "bm_in": np.ascontiguousarray(a["bm"]),
    }
    nc = bacc.Bacc("TRN2", target_bir_lowering=False, num_devices=1)
    d = {k: nc.dram_tensor(k, v.shape, F32, kind="ExternalInput").ap() for k, v in arrays.items()}
    out = nc.dram_tensor("out_tiles", (NC, P, JT, D), F32, kind="ExternalOutput").ap()

    def spread(ap):
        return ap.rearrange("(a n) -> a n", a=1).to_broadcast([P, ap.shape[0]])

    two_layer_graph_kernel(nc, d["adj_blocks"], d["xs_tiles"], d["pack_w"], d["w_dt_rows"],
                           spread(d["eps1_in"]), spread(d["eps2_in"]), spread(d["bm_in"]), out)
    res = run(nc, [arrays], core_ids=[0])
    got = res.results[0]["out_tiles"]
    return np.ascontiguousarray(got.transpose(0, 2, 1, 3).reshape(N, D))
```
